# Optimizing a Trainium2 kernel written in Bass

```python
import numpy as np
import jax
import jax.numpy as jnp

def _softmax(x, axis=-1):
    return jax.nn.softmax(x, axis=axis)

def _gelu(x):
    return jax.nn.gelu(x, approximate=True)

def _silu(x):
    return jax.nn.silu(x)

def _sigmoid(x):
    return jax.nn.sigmoid(x)

def _layernorm(x, axis=-1, eps=1e-05):
    m = jnp.mean(x, axis=axis, keepdims=True)
    v = jnp.var(x, axis=axis, keepdims=True)
    return (x - m) / jnp.sqrt(v + eps)

def _scatter_add(tgt, idx, src, axis=0):
    return tgt.at[idx].add(src)

def _segment_sum(src, seg, n):
    return jax.ops.segment_sum(src, seg, n)
kernel_name = 'mk_gnn_resnorm_d4_gnn_r64_47b4f7'

def setup_inputs(seed: int=0):
    np.random.seed(seed)
    _w = jnp.asarray

    def _rec_inputs():
        import jax
        import jax.numpy as jnp
        _gk = jax.random.key(seed)
        x = -0.000202 + 1 * jax.random.normal(jax.random.fold_in(_gk, 1), (50000, 128), jnp.float32)
        src = jax.random.randint(jax.random.fold_in(_gk, 2), (25000,), 0, 50000, jnp.int32)
        dst = jax.random.randint(jax.random.fold_in(_gk, 3), (25000,), 0, 50000, jnp.int32)
        _o = jnp.argsort(dst, stable=True)
        src = src[_o]
        dst = dst[_o]
        edge_attr_128 = -4.21973e-05 + 0.999841 * jax.random.normal(jax.random.fold_in(_gk, 11), (25000, 128), jnp.float32)
        edge_type_10 = jax.random.randint(jax.random.fold_in(_gk, 13), (25000,), 0, 10, jnp.int32)
        return (x, src, dst, edge_attr_128, edge_type_10)
    x, src, dst, edge_attr_128, edge_type_10 = _rec_inputs()

    def _L0_gnn_setup():
        import jax, jax.numpy as jnp
        import numpy as np
        N_NODES = 50000
        N_EDGES = 9375
        IN_DIM = 128
        OUT_DIM = 128
        N_REL = 10
        LN_EPS = 1e-05
        key = jax.random.key(seed)
        ks = jax.random.split(key, 6)
        x = jax.random.normal(ks[0], (N_NODES, IN_DIM), dtype=jnp.float32)
        edge_index = jax.random.randint(ks[1], (2, N_EDGES), 0, N_NODES, dtype=jnp.int64)
        edge_type = jax.random.randint(ks[2], (N_EDGES,), 0, N_REL, dtype=jnp.int64)
        limit = float(np.sqrt(6.0 / (IN_DIM + OUT_DIM)))
        relation_weights = jax.random.uniform(ks[3], (N_REL, IN_DIM, OUT_DIM), minval=-limit, maxval=limit, dtype=jnp.float32)
        relation_bias = jnp.zeros((N_REL, OUT_DIM), dtype=jnp.float32)
        bound = float(1.0 / np.sqrt(IN_DIM))
        w_self = jax.random.uniform(ks[4], (OUT_DIM, IN_DIM), minval=-bound, maxval=bound, dtype=jnp.float32)
        b_self = jax.random.uniform(ks[5], (OUT_DIM,), minval=-bound, maxval=bound, dtype=jnp.float32)
        ln_gamma = jnp.ones((OUT_DIM,), dtype=jnp.float32)
        ln_beta = jnp.zeros((OUT_DIM,), dtype=jnp.float32)
        return {'x': x, 'edge_index': edge_index, 'edge_type': edge_type, 'relation_weights': relation_weights, 'relation_bias': relation_bias, 'w_self': w_self, 'b_self': b_self, 'ln_gamma': ln_gamma, 'ln_beta': ln_beta}
    _L0_gnn_all = _L0_gnn_setup()
    _L0_gnn_in = {k: v for k, v in _L0_gnn_all.items() if k in ('relation_weights', 'relation_bias', 'w_self', 'b_self', 'ln_gamma', 'ln_beta')}
    del _L0_gnn_all

    def _L1_gnn_setup():
        import jax, jax.numpy as jnp
        import numpy as np
        N_NODES = 100000
        N_EDGES = 10000
        DIM = 128
        key = jax.random.key(seed)
        k1, k2, k3, k4 = jax.random.split(key, 4)
        x = jax.random.normal(k1, (N_NODES, DIM), dtype=jnp.float32)
        edge_index = jax.random.randint(k2, (2, N_EDGES), 0, N_NODES, dtype=jnp.int64)
        W = jax.random.normal(k3, (DIM, DIM), dtype=jnp.float32) / jnp.sqrt(jnp.float32(DIM))
        b = jax.random.normal(k4, (DIM,), dtype=jnp.float32) * 0.01
        return {'x': x, 'edge_index': edge_index, 'W': W, 'b': b}
    _L1_gnn_all = _L1_gnn_setup()
    _L1_gnn_in = {k: v for k, v in _L1_gnn_all.items() if k in ('W', 'b')}
    del _L1_gnn_all

    def _L2_gnn_setup():
        import jax, jax.numpy as jnp
        import numpy as np
        N_NODES = 50000
        N_EDGES = 12500
        IN_CH = 128
        OUT_CH = 128
        MLP_HID = 64
        key = jax.random.key(seed)
        ks = jax.random.split(key, 8)
        x = jax.random.normal(ks[0], (N_NODES, IN_CH), dtype=jnp.float32)
        edge_index = jax.random.randint(ks[1], (2, N_EDGES), 0, N_NODES, dtype=jnp.int64)
        s1 = 1.0 / np.sqrt(2 * IN_CH)
        mlp_w1 = jax.random.uniform(ks[2], (2 * IN_CH, MLP_HID), jnp.float32, -s1, s1)
        mlp_b1 = jax.random.uniform(ks[3], (MLP_HID,), jnp.float32, -s1, s1)
        s2 = 1.0 / np.sqrt(MLP_HID)
        mlp_w2 = jax.random.uniform(ks[4], (MLP_HID, 1), jnp.float32, -s2, s2)
        mlp_b2 = jax.random.uniform(ks[5], (1,), jnp.float32, -s2, s2)
        s3 = 1.0 / np.sqrt(IN_CH)
        conv_w = jax.random.uniform(ks[6], (IN_CH, OUT_CH), jnp.float32, -s3, s3)
        conv_b = jnp.zeros((OUT_CH,), jnp.float32)
        return {'x': x, 'edge_index': edge_index, 'mlp_w1': mlp_w1, 'mlp_b1': mlp_b1, 'mlp_w2': mlp_w2, 'mlp_b2': mlp_b2, 'conv_w': conv_w, 'conv_b': conv_b}
    _L2_gnn_all = _L2_gnn_setup()
    _L2_gnn_in = {k: v for k, v in _L2_gnn_all.items() if k in ('mlp_w1', 'mlp_b1', 'mlp_w2', 'mlp_b2', 'conv_w', 'conv_b')}
    del _L2_gnn_all

    def _L3_gnn_setup():
        import jax, jax.numpy as jnp
        import numpy as np
        N_NODES = 50000
        N_EDGES = 9375
        D = 128
        NUM_LAYERS = 2
        ALPHA = 0.5
        EPS = 1e-12
        key = jax.random.key(seed)
        k1, k2, k3, k4, k5 = jax.random.split(key, 5)
        x = jax.random.normal(k1, (N_NODES, D), dtype=jnp.float32)
        edge_attr = jax.random.normal(k2, (N_EDGES, D), dtype=jnp.float32)
        question_emb = jax.random.normal(k3, (D,), dtype=jnp.float32)
        src = jax.random.randint(k4, (N_EDGES,), 0, N_NODES)
        dst = jax.random.randint(k5, (N_EDGES,), 0, N_NODES)
        edge_index = jnp.stack([src, dst], axis=0).astype(jnp.int64)
        return {'x': x, 'edge_attr': edge_attr, 'question_emb': question_emb, 'edge_index': edge_index}
    _L3_gnn_all = _L3_gnn_setup()
    _L3_gnn_in = {k: v for k, v in _L3_gnn_all.items() if k in ('question_emb',)}
    del _L3_gnn_all
    return {'x': x, 'src': src, 'dst': dst, 'edge_attr_128': edge_attr_128, 'edge_type_10': edge_type_10, 'L0_gnn_relation_weights': _L0_gnn_in['relation_weights'], 'L0_gnn_relation_bias': _L0_gnn_in['relation_bias'], 'L0_gnn_w_self': _L0_gnn_in['w_self'], 'L0_gnn_b_self': _L0_gnn_in['b_self'], 'L0_gnn_ln_gamma': _L0_gnn_in['ln_gamma'], 'L0_gnn_ln_beta': _L0_gnn_in['ln_beta'], 'L1_gnn_W': _L1_gnn_in['W'], 'L1_gnn_b': _L1_gnn_in['b'], 'L2_gnn_mlp_w1': _L2_gnn_in['mlp_w1'], 'L2_gnn_mlp_b1': _L2_gnn_in['mlp_b1'], 'L2_gnn_mlp_w2': _L2_gnn_in['mlp_w2'], 'L2_gnn_mlp_b2': _L2_gnn_in['mlp_b2'], 'L2_gnn_conv_w': _L2_gnn_in['conv_w'], 'L2_gnn_conv_b': _L2_gnn_in['conv_b'], 'L3_gnn_question_emb': _L3_gnn_in['question_emb']}

def reference(x, src, dst, edge_attr_128, edge_type_10, L0_gnn_relation_weights, L0_gnn_relation_bias, L0_gnn_w_self, L0_gnn_b_self, L0_gnn_ln_gamma, L0_gnn_ln_beta, L1_gnn_W, L1_gnn_b, L2_gnn_mlp_w1, L2_gnn_mlp_b1, L2_gnn_mlp_w2, L2_gnn_mlp_b2, L2_gnn_conv_w, L2_gnn_conv_b, L3_gnn_question_emb):
    import jax
    import jax.numpy as jnp

    def _L0_gnn_ref(x, edge_index, edge_type, relation_weights, relation_bias, w_self, b_self, ln_gamma, ln_beta):
        import jax, jax.numpy as jnp
        import numpy as np
        N_NODES = 50000
        N_EDGES = 9375
        IN_DIM = 128
        OUT_DIM = 128
        N_REL = 10
        LN_EPS = 1e-05
        num_nodes = x.shape[0]
        out = x @ w_self.T + b_self
        xr = jnp.einsum('nd,rdo->rno', x, relation_weights)
        src, dst = (edge_index[0], edge_index[1])
        messages = xr[edge_type, src] + relation_bias[edge_type]
        out = out + jax.ops.segment_sum(messages, dst, num_segments=num_nodes)
        mean = jnp.mean(out, axis=-1, keepdims=True)
        var = jnp.mean(jnp.square(out - mean), axis=-1, keepdims=True)
        return (out - mean) * jax.lax.rsqrt(var + LN_EPS) * ln_gamma + ln_beta

    def _L1_gnn_ref(x, edge_index, W, b):
        import jax, jax.numpy as jnp
        import numpy as np
        N_NODES = 100000
        N_EDGES = 10000
        DIM = 128
        src = edge_index[0]
        dst = edge_index[1]
        agg = jax.ops.segment_sum(x[src], dst, num_segments=x.shape[0])
        h = (x + agg) @ W + b
        return jax.nn.relu(h)

    def _L2_gnn_ref(x, edge_index, mlp_w1, mlp_b1, mlp_w2, mlp_b2, conv_w, conv_b):
        import jax, jax.numpy as jnp
        import numpy as np
        N_NODES = 50000
        N_EDGES = 12500
        IN_CH = 128
        OUT_CH = 128
        MLP_HID = 64
        n = x.shape[0]
        row, col = (edge_index[0], edge_index[1])
        edge_feat = jnp.concatenate([x[row], x[col]], axis=-1)
        h = jax.nn.gelu(edge_feat @ mlp_w1 + mlp_b1, approximate=False)
        edge_weight = jax.nn.sigmoid(h @ mlp_w2 + mlp_b2)[:, 0]
        loop = jnp.arange(n, dtype=row.dtype)
        row_f = jnp.concatenate([row, loop])
        col_f = jnp.concatenate([col, loop])
        ew_f = jnp.concatenate([edge_weight, jnp.ones((n,), x.dtype)])
        deg = jax.ops.segment_sum(ew_f, col_f, num_segments=n)
        dinv = jnp.where(deg > 0, jax.lax.rsqrt(deg), 0.0)
        norm = dinv[row_f] * ew_f * dinv[col_f]
        xt = x @ conv_w
        msg = xt[row_f] * norm[:, None]
        out = jax.ops.segment_sum(msg, col_f, num_segments=n)
        return out + conv_b

    def _L3_gnn_ref(x, edge_attr, question_emb, edge_index):
        import jax, jax.numpy as jnp
        import numpy as np
        N_NODES = 50000
        N_EDGES = 9375
        D = 128
        NUM_LAYERS = 2
        ALPHA = 0.5
        EPS = 1e-12
        num_nodes = x.shape[0]
        ea = edge_attr / jnp.maximum(jnp.linalg.norm(edge_attr, axis=1, keepdims=True), EPS)
        q = question_emb / jnp.maximum(jnp.linalg.norm(question_emb), EPS)
        edge_sim = ea @ q
        src, dst = (edge_index[0], edge_index[1])
        deg = jax.ops.segment_sum(jnp.ones_like(edge_sim), dst, num_segments=num_nodes)
        deg = jnp.clip(deg, 1.0)[:, None]
        for _ in range(NUM_LAYERS):
            msgs = x[src] * edge_sim[:, None]
            x_new = jax.ops.segment_sum(msgs, dst, num_segments=num_nodes)
            x_new = x_new / deg
            x = ALPHA * x + (1.0 - ALPHA) * x_new
        return x
    edge_index = jnp.stack([src, dst])
    x = _layernorm(x + _L0_gnn_ref(x, edge_index, edge_type_10, L0_gnn_relation_weights, L0_gnn_relation_bias, L0_gnn_w_self, L0_gnn_b_self, L0_gnn_ln_gamma, L0_gnn_ln_beta), axis=-1)
    x = _layernorm(x + _L1_gnn_ref(x, edge_index, L1_gnn_W, L1_gnn_b), axis=-1)
    x = _layernorm(x + _L2_gnn_ref(x, edge_index, L2_gnn_mlp_w1, L2_gnn_mlp_b1, L2_gnn_mlp_w2, L2_gnn_mlp_b2, L2_gnn_conv_w, L2_gnn_conv_b), axis=-1)
    x = _layernorm(x + _L3_gnn_ref(x, edge_attr_128, L3_gnn_question_emb, edge_index), axis=-1)
    return x

_drawn_inputs = setup_inputs


def setup_inputs(seed=0):
    import zlib

    import numpy as np

    out = dict(_drawn_inputs(seed))
    spreads = {'L0_gnn_relation_bias': (0.0, 0.1),
     'L0_gnn_ln_gamma': (1.0, 0.2),
     'L0_gnn_ln_beta': (0.0, 0.1),
     'L2_gnn_conv_b': (0.0, 0.1)}
    factors = {'edge_attr_128': 8.048,
     'L1_gnn_b': 8.0,
     'L2_gnn_mlp_w1': 5.154,
     'L2_gnn_mlp_b1': 32.185,
     'L2_gnn_mlp_w2': 4.777,
     'L3_gnn_question_emb': 8.173}
    for name, (base, spread) in spreads.items():
        noise = np.random.default_rng([zlib.crc32(name.encode()), seed]).standard_normal(out[name].shape)
        drawn = base * np.exp(spread * noise) if base else spread * noise
        out[name] = jnp.asarray(drawn.astype(out[name].dtype))
    for name, factor in factors.items():
        out[name] = (out[name] * factor).astype(out[name].dtype)
    return out
```

```python
import concourse.bass as bass
from concourse import mybir
from contextlib import ExitStack


def gnn_kernel(nc, x, src, dst, edge_attr, edge_type, rel_w, rel_b, w_self, b_self, ln_g, ln_b,
               w1, b1, mlp_w1, mlp_b1, mlp_w2, mlp_b2, conv_w, conv_b, q_emb, out):
    f32, i32 = mybir.dt.float32, mybir.dt.int32
    ALU, ACT, AX = mybir.AluOpType, mybir.ActivationFunctionType, mybir.AxisListType
    N, D = x.shape
    E = src.shape[0]
    R = rel_w.shape[0]
    H = mlp_w1.shape[1]
    P, J, K = 128, 3, 2
    GN, GE = P * J, P * K
    NG = -(-N // GN)
    NPAD = NG * GN
    RING = 8
    LAST = N - (NG - 1) * GN
    EP, EC, EB = 125, E // 125, 8
    NB = EC // EB
    REL_CUT = ((0, 3), (3, 6), (6, R))
    NW = 20
    EPS_LN, EPS_Q = 1e-5, 1e-12

    ctx = ExitStack()
    with ctx:
        def sb(name, shape, dt=f32):
            return ctx.enter_context(nc.sbuf_tensor(name, shape, dt))

        def sem(name):
            return ctx.enter_context(nc.semaphore(name))

        def dram(name, rows, cols, dt=f32):
            return nc.dram_tensor(name, (rows, cols), dt, kind="Internal").ap()

        msg0 = dram("msg0", E + GE, D)
        rec = dram("rec", E + GE, 4, i32)
        win = dram("win", NG * GE, 4, i32)
        x1 = dram("x1", NPAD, D)
        x2 = dram("x2", NPAD, D)
        x2s = dram("x2s", NPAD, D)
        x3 = dram("x3", NPAD, D)
        h1 = dram("h1", NPAD, D)

        ident = sb("ident", [P, P])
        node_iota = sb("node_iota", [P, J, P])
        group_base = sb("group_base", [P, NG])
        rel_iota = sb("rel_iota", [P, R])
        ones_row = sb("ones_row", [1, P])
        ones_col = sb("ones_col", [P, 1])
        eps_col = sb("eps_col", [P, 1])
        zero_pad = sb("zero_pad", [P, K * D])
        rec_pad = sb("rec_pad", [P, K, 4], i32)
        w_rel = sb("w_rel", [D, R * D])
        b_rel = sb("b_rel", [R, D])
        w_raw = sb("w_raw", [D, D])
        w_selfT = sb("w_selfT", [D, D])
        b_self_row = sb("b_self_row", [1, J, D])
        b1_row = sb("b1_row", [1, J, D])
        gam = sb("gam", [P, D])
        bet = sb("bet", [P, D])
        w1_sb = sb("w1_sb", [D, D])
        mw1 = sb("mw1", [D, 2, H])
        mb1 = sb("mb1", [H, 1])
        mw2 = sb("mw2", [H, 1])
        mb2 = sb("mb2", [P, 1])
        mb2h = sb("mb2h", [P, 1])
        cw = sb("cw", [D, D])
        cb = sb("cb", [P, D])
        qb = sb("qb", [P, D])
        qsq = sb("qsq", [P, D])
        qn = sb("qn", [P, 4])

        src_n = sb("src_n", [EP, EC], i32)
        dst_n = sb("dst_n", [EP, EC], i32)
        typ_n = sb("typ_n", [EP, EC], i32)
        dstf = sb("dstf", [EP, EC])
        typf = sb("typf", [EP, EC])
        dotq = sb("dotq", [EP, EC])
        ssq = sb("ssq", [EP, EC])
        rec_n = sb("rec_n", [EP, EC, 4], i32)
        rel_1h = sb("rel_1h", [EP, EC, R])
        CB = 11
        picks = sb("picks", [EP, 2 * (R + 1) * D])
        cmp_t = picks[:, 0:CB * EC].rearrange("p (b c) -> p b c", b=CB)
        sel = picks[:, :].rearrange("p (c r d) -> p c r d", c=2, r=R + 1)
        cnt = sb("cnt", [EP, NG])
        e0_row = sb("e0_row", [1, NG], i32)
        attr = sb("attr", [EP, 2, EB * D])
        prod = sb("prod", [EP, 2, EB * D])
        prod2 = sb("prod2", [EP, 2, EB * D])
        nrm = sb("nrm", [EP, EC])
        idx_b = sb("idx_b", [EP, 2, EB], i32)
        gat = sb("gat", [EP, 4, D])
        gatT = sb("gatT", [D, 2, EP])
        rohT = sb("rohT", [R, 2, EP])
        roh = sb("roh", [EP, 2, EB, R])
        msum = sb("msum", [EP, 2, EB, D])

        xa = sb("xa", [P, RING, J, D])
        xb = sb("xb", [P, RING, J, D])
        wrec = sb("wrec", [P, RING, K, 4], i32)
        G = sb("G", [P, RING, K, D])
        S = sb("S", [P, RING, K, J, P])
        drel = sb("drel", [P, RING, K])
        y = sb("y", [P, 4, J, D])
        yT = sb("yT", [P, 4, J, D])
        r = sb("r", [P, 4, J, D])
        st6a = sb("st6a", [P, 4, J, 6])
        mva = sb("mva", [P, 4, J, 2])
        sda = sb("sda", [P, 4, J])
        rsa = sb("rsa", [P, 4, J])
        nba = sb("nba", [P, 4, J])
        st6b = sb("st6b", [P, 4, J, 6])
        mvb = sb("mvb", [P, 4, J, 2])
        sdb = sb("sdb", [P, 4, J])
        rsb = sb("rsb", [P, 4, J])
        nbb = sb("nbb", [P, 4, J])
        o = sb("o", [P, 4, J, D])
        hx = sb("hx", [P, 4, J, D])
        ew_tab = sb("ew_tab", [P, NG, K])
        dinv_tab = sb("dinv_tab", [P, NG, J])
        chalf_tab = sb("chalf_tab", [P, NG, J])
        gT = sb("gT", [D, 4, K, P])
        sT = sb("sT", [P, 2, K, J, P])
        xdT = sb("xdT", [D, 4, K, P])
        hh = sb("hh", [H, 4, K, P])
        ew1 = sb("ew1", [P, 4, K, 2])
        th = sb("th", [P, 4, K])
        dg = sb("dg", [P, 2, J, 2])
        ny = sb("ny", [P, 2, J])
        na = sb("na", [P, 2, J])
        nd = sb("nd", [P, 2, J])

        bank = [ctx.enter_context(nc.psum_tensor(f"bank{i}", [P, 512], f32)) for i in range(8)]

        def bj(i):
            return bank[i][:, 0:J * D].rearrange("p (j d) -> p j d", j=J)

        class PerGroup:

            def __init__(self, name, passes, per=1):
                self.sem, self.passes, self.per = sem(name), passes, per

            def at(self, p, g, k=None):
                return ((g + self.passes.index(p) * NG) * self.per) + (self.per if k is None else k)

        weights_in = sem("weights_in")
        edges_in = sem("edges_in")
        consts = sem("consts")
        dve_own = sem("dve_own")
        act_own = sem("act_own")
        cnt_done = sem("cnt_done")
        sums_done = sem("sums_done")
        rec_done = sem("rec_done")
        roots_done = sem("roots_done")
        e0_sum = sem("e0_sum")
        wsT_done = sem("wsT_done")
        wsT_copied = sem("wsT_copied")
        e0_ready = sem("e0_ready")
        attr_in = [sem(f"attr_in{i}") for i in range(2)]
        attr_mul = sem("attr_mul")
        attr_sq = sem("attr_sq")
        sum_used = sem("sum_used")
        pads_out = sem("pads_out")
        rec_out = sem("rec_out")
        idx_ready = sem("idx_ready")
        gat_in = [sem(f"gat_in{i}") for i in range(4)]
        gat_started = sem("gat_started")
        roh_ready = sem("roh_ready")
        msg_T = sem("msg_T")
        msg_Tc = sem("msg_Tc")
        msg_Z = sem("msg_Z")
        msg_act = sem("msg_act")
        msg_sel = sem("msg_sel")
        msg_sum = sem("msg_sum")
        msg_out = [sem(f"msg_out{i}") for i in range(2)]
        xa_in = [sem(f"xa_in{i}") for i in range(RING)]
        xb_in = [sem(f"xb_in{i}") for i in range(RING)]
        rec_in = [sem(f"rec_in{i}") for i in range(RING)]
        M_in = [sem(f"M_in{i}") for i in range(RING)]
        G_in = [sem(f"G_in{i}") for i in range(RING)]
        stored = [sem(f"stored{i}") for i in range(4)]
        win_out = sem("win_out")
        aggr_started = sem("aggr_started")
        slot_free = sem("slot_free")
        table_ready = sem("table_ready")
        ALLP = (0, 1, 2, 3, 4, 5)
        drel_done = PerGroup("drel_done", ALLP)
        S_done = PerGroup("S_done", ALLP)
        agg_done = PerGroup("agg_done", (1, 3, 4, 5))
        y_done = PerGroup("y_done", (1, 3))
        T_done = PerGroup("T_done", (0, 1, 2, 3))
        Tc_done = PerGroup("Tc_done", (0, 1, 2, 3))
        H_done = PerGroup("H_done", (0, 1, 3))
        sum_done = PerGroup("sum_done", (1, 3, 5))
        mid_done = PerGroup("mid_done", (0,), 3)
        base_done = PerGroup("base_done", (3, 5))
        half_done = PerGroup("half_done", (4,))
        bn_done = PerGroup("bn_done", (0, 1, 3, 5))
        var_done = PerGroup("var_done", (0, 1, 3, 5))
        sd_done = PerGroup("sd_done", (0, 1, 3, 5))
        rs_done = PerGroup("rs_done", (0, 1, 3, 5))
        nb_done = PerGroup("nb_done", (0, 1, 3, 5))
        bn0_done = PerGroup("bn0_done", (0,))
        var0_done = PerGroup("var0_done", (0,))
        sd0_done = PerGroup("sd0_done", (0,))
        rs0_done = PerGroup("rs0_done", (0,))
        nb0_done = PerGroup("nb0_done", (0,))
        n0_done = PerGroup("n0_done", (0,))
        o_done = PerGroup("o_done", ALLP)
        sTc_done = PerGroup("sTc_done", (2,))
        xd_done = PerGroup("xd_done", (2,))
        xdc_done = PerGroup("xdc_done", (2,))
        hp_done = PerGroup("hp_done", (2,))
        hh_done = PerGroup("hh_done", (2,))
        ep_done = PerGroup("ep_done", (2,))
        th_done = PerGroup("th_done", (2,))
        ew_done = PerGroup("ew_done", (2,))
        dg_done = PerGroup("dg_done", (2,))
        NEWTON = 3
        di_done = PerGroup("di_done", (2,), 7 + 3 * NEWTON)

        def uses(u, ring):
            return (NG - u + ring - 1) // ring

        def run_steps(eng, stages):
            top = NG - 1 + max(lag for lag, _ in stages)
            blocks = (NG - 1) // RING
            for s in range(RING):
                for lag, stage in stages:
                    if s >= lag:
                        stage(s - lag, (s - lag) % RING, (s - lag) // RING)
            with eng.Fori(1, blocks) as i:
                for s in range(RING):
                    for lag, stage in stages:
                        stage(i * RING + (s - lag), (s - lag) % RING, i + (s - lag) // RING)
            for s in range(blocks * RING, top + 1):
                for lag, stage in stages:
                    if 0 <= s - lag < NG:
                        stage(s - lag, (s - lag) % RING, (s - lag) // RING)

        def run_batches(eng, batch):
            batch(0, 0, 0)
            batch(1, 1, 0)
            with eng.Fori(1, NB // 2) as i:
                for par in range(2):
                    batch(i * 2 + par, par, i)
            batch(NB - 1, 0, NB // 2)

        def cut(g, size):
            return slice(g * size, (g + 1) * size) if isinstance(g, int) else bass.ds(g * size, size)

        def early(g, k):
            return isinstance(g, int) and g < k

        PASS = [dict(gather=None, a=x, b=None, out=x1),
                dict(gather=x1, a=x1, b=None, out=x2),
                dict(gather=x2, a=x2, b=None, out=x2s),
                dict(gather=x2s, a=x2s, b=x2, out=x3),
                dict(gather=x3, a=x3, b=None, out=h1),
                dict(gather=h1, a=h1, b=x3, out=out)]
        STORE_LAG = 8

        def rec_count(p, u, n):
            return (n + p * uses(u, RING)) * 16 + 16

        def G_count(p, u, n):
            return (n + (p - 1) * uses(u, RING)) * 16 * K + 16 * K

        def xa_count(p, u, n):
            tail = 16 if u == (NG - 1) % RING and (p > 0 or (isinstance(n, int) and n == NG // RING)) else 0
            return (n + p * uses(u, RING)) * 16 + 16 + tail

        def xb_count(p, u, n):
            return (n + {3: 0, 5: 1}[p] * uses(u, RING)) * 16 + 16

        def stored_before(p, u, n):
            return (n * 2 + u // 4 + p * uses(u % 4, 4)) * 16

        def flat(ring, u):
            return ring[:, u, :, :].rearrange("p j d -> p (j d)")

        def col(table, g):
            return table[:, g, :] if isinstance(g, int) else table[:, bass.ds(g, 1), :].rearrange("p a w -> p (a w)")

        def cell(table, g, j):
            return table[:, g, j:j + 1] if isinstance(g, int) else table[:, bass.ds(g, 1), j]

        block = ctx.enter_context(nc.Block())

        @block.sync
        def _(sp):
            sp.dma_start(src_n[:, :], src.rearrange("(p c) -> p c", p=EP)).then_inc(edges_in, 16)
            sp.dma_start(dst_n[:, :], dst.rearrange("(p c) -> p c", p=EP)).then_inc(edges_in, 16)
            sp.dma_start(typ_n[:, :], edge_type.rearrange("(p c) -> p c", p=EP)).then_inc(edges_in, 16)

            def row(v):
                return v.rearrange("(a n) -> a n", a=1)

            loads = [(w_rel[:, :].rearrange("d (r o) -> d r o", r=R), rel_w.rearrange("r d o -> d r o")),
                     (b_rel[:, :], rel_b), (w_raw[:, :], w_self),
                     (gam[:, :], row(ln_g).to_broadcast((P, D))), (bet[:, :], row(ln_b).to_broadcast((P, D))),
                     (w1_sb[:, :], w1), (mw1[:, 0, :], mlp_w1[0:D, :]), (mw1[:, 1, :], mlp_w1[D:2 * D, :]),
                     (mb1[:, :], mlp_b1.rearrange("(n a) -> n a", a=1)), (mw2[:, :], mlp_w2),
                     (mb2[:, :], row(mlp_b2).to_broadcast((P, 1))), (cw[:, :], conv_w),
                     (cb[:, :], row(conv_b).to_broadcast((P, D))), (qb[:, :], row(q_emb).to_broadcast((P, D)))]
            for j in range(J):
                loads += [(b_self_row[0:1, j, :], row(b_self)), (b1_row[0:1, j, :], row(b1))]
            assert len(loads) == NW
            for to, fro in loads:
                sp.dma_start(to, fro).then_inc(weights_in, 16)

            sp.wait_ge(consts, 1)
            sp.dma_start(msg0[E:E + GE, :].rearrange("(p k) d -> p (k d)", k=K), zero_pad[:, :]).then_inc(pads_out, 16)
            sp.dma_start(rec[E:E + GE, :].rearrange("(p k) d -> p (k d)", k=K),
                         rec_pad[:, :, :].rearrange("p k d -> p (k d)")).then_inc(pads_out, 16)

            attr_v = edge_attr.rearrange("(p c) d -> p (c d)", p=EP)

            def attr_batch(b, par, n):
                if not early(b, 2):
                    sp.wait_ge(attr_mul, b - 1)
                    sp.wait_ge(attr_sq, b - 1)
                for lo, hi in ((0, 112), (112, EP)):
                    sp.dma_start(attr[lo:hi, par, :], attr_v[lo:hi, cut(b, EB * D)]).then_inc(attr_in[par], 16)

            run_batches(sp, attr_batch)
            sp.wait_ge(rec_done, 1)
            sp.dma_start(rec[0:E, :].rearrange("(p c) d -> p (c d)", p=EP),
                         rec_n[:, :, :].rearrange("p c d -> p (c d)")).then_inc(rec_out, 16)

            def msg_batch(b, par, n):
                sp.wait_ge(msg_sum, b * EB + EB)
                sp.dma_start(msg0[0:E, :].rearrange("(p c) d -> p (c d)", p=EP)[:, cut(b, EB * D)],
                             msum[:, par, :, :].rearrange("p c d -> p (c d)")).then_inc(msg_out[par], 16)

            run_batches(sp, msg_batch)
            sp.wait_ge(msg_out[0], 16 * (NB - NB // 2))
            sp.wait_ge(msg_out[1], 16 * (NB // 2))
            sp.wait_ge(rec_out, 16)
            sp.wait_ge(pads_out, 32)
            sp.wait_ge(e0_ready, 1)

            full, rest = LAST // J, LAST % J

            for p, ps in enumerate(PASS):
                def load(g, u, n, p=p, ps=ps):
                    last = isinstance(g, int) and g == NG - 1
                    if not early(g, RING):
                        sp.wait_ge(o_done.sem, o_done.at(p, g - RING))
                        sp.sem_inc(slot_free, 1)
                    if p == 0:
                        e0 = sp.value_load(e0_row[0:1, cut(g, 1)], min_val=0, max_val=E)
                        window = rec[bass.ds(e0, GE), :].rearrange("(p k) f -> p (k f)", k=K)
                        sp.dma_start(wrec[:, u, :, :].rearrange("p k f -> p (k f)"), window).then_inc(rec_in[u], 16)
                        sp.dma_start(flat(G, u), msg0[bass.ds(e0, GE), :].rearrange("(p k) d -> p (k d)", k=K)).then_inc(M_in[u], 16)
                        sp.dma_start(win[cut(g, GE), :].rearrange("(p k) f -> p (k f)", k=K), window).then_inc(win_out, 16)
                    else:
                        sp.dma_start(wrec[:, u, :, :].rearrange("p k f -> p (k f)"),
                                     win[cut(g, GE), :].rearrange("(p k) f -> p (k f)", k=K)).then_inc(rec_in[u], 16)
                    if p == 0 and last:
                        r0 = g * GN
                        sp.dma_start(flat(xa, u)[0:full, :], x[r0:r0 + full * J, :].rearrange("(p j) d -> p (j d)", j=J)).then_inc(xa_in[u], 16)
                        sp.dma_start(flat(xa, u)[full:full + 1, 0:rest * D],
                                     x[r0 + full * J:N, :].rearrange("(p j) d -> p (j d)", j=rest)).then_inc(xa_in[u], 16)
                    else:
                        sp.dma_start(flat(xa, u), ps["a"][cut(g, GN), :].rearrange("(p j) d -> p (j d)", j=J)).then_inc(xa_in[u], 16)
                    if ps["b"] is not None:
                        sp.dma_start(flat(xb, u), ps["b"][cut(g, GN), :].rearrange("(p j) d -> p (j d)", j=J)).then_inc(xb_in[u], 16)

                def store(g, u, n, p=p, ps=ps):
                    sp.wait_ge(o_done.sem, o_done.at(p, g))
                    rows = flat(o, u % 4)
                    if p == len(PASS) - 1 and isinstance(g, int) and g == NG - 1:
                        r0 = g * GN
                        sp.dma_start(out[r0:r0 + full * J, :].rearrange("(p j) d -> p (j d)", j=J), rows[0:full, :]).then_inc(stored[u % 4], 16)
                        sp.dma_start(out[r0 + full * J:N, :].rearrange("(p j) d -> p (j d)", j=rest),
                                     rows[full:full + 1, 0:rest * D]).then_inc(stored[u % 4], 16)
                    else:
                        sp.dma_start(ps["out"][cut(g, GN), :].rearrange("(p j) d -> p (j d)", j=J), rows).then_inc(stored[u % 4], 16)

                run_steps(sp, [(STORE_LAG, store), (0, load)])
                for q in range(4):
                    tail = 16 if p == len(PASS) - 1 and (NG - 1) % 4 == q else 0
                    sp.wait_ge(stored[q], 16 * (p + 1) * uses(q, 4) + tail)
                if p == 0:
                    sp.wait_ge(win_out, 16 * NG)
                sp.sem_inc(table_ready, 1)

        @block.gpsimd
        def _(pool):
            nc.gpsimd.memset(zero_pad[:, :], 0.0)
            nc.gpsimd.memset(rec_pad[:, :, 0:1], 0)
            nc.gpsimd.memset(rec_pad[:, :, 1:2].bitcast(f32), -1.0)
            nc.gpsimd.memset(rec_pad[:, :, 2:4], 0).then_inc(consts, 1)
            nc.gpsimd.memset(rec_n[:, :, 3:4], 0)
            nc.gpsimd.memset(ident[:, :], 0.0)
            nc.gpsimd.memset(ones_row[:, :], 1.0)
            nc.gpsimd.memset(ones_col[:, :], 1.0)
            nc.gpsimd.memset(eps_col[:, :], EPS_LN)
            nc.gpsimd.memset(ew1[:, :, :, 1:2], 1.0)
            nc.gpsimd.iota(node_iota[:, :, :], pattern=[[1, J], [J, P]], base=0, channel_multiplier=0, allow_small_or_imprecise_dtypes=True)
            nc.gpsimd.iota(group_base[:, :], pattern=[[GN, NG]], base=0, channel_multiplier=0, allow_small_or_imprecise_dtypes=True)
            nc.gpsimd.iota(rel_iota[:, :], pattern=[[1, R]], base=0, channel_multiplier=0, allow_small_or_imprecise_dtypes=True).then_inc(consts, 1)
            pool.wait_ge(consts, 2)
            nc.gpsimd.affine_select(out=ident[:, :], in_=ident[:, :], compare_op=ALU.not_equal, fill=1.0, base=0,
                                    pattern=[[-1, P]], channel_multiplier=1).then_inc(consts, 1)

            pool.wait_ge(edges_in, 48)

            def gather_batch(b, par, n):
                if not early(b, 1):
                    for q in range(4):
                        pool.wait_ge(gat_in[q], b * (16 * EB // 4))
                nc.gpsimd.tensor_copy(idx_b[:, par, :], src_n[:, cut(b, EB)]).then_inc(idx_ready, 1)
                for c in range(EB):
                    if c == 0:
                        pool.wait_ge(idx_ready, b + 1)
                    if not (early(b, 1) and c < 4):
                        pool.wait_ge(msg_T, b * EB + (c - 3))
                    pool.sem_inc(gat_started, 1)
                    pool.indirect_dma_start(gat[:, c % 4, :], None, x, bass.IndirectOffsetOnAxis(
                        ap=idx_b[:, par, c:c + 1], axis=0)).then_inc(gat_in[c % 4], 16)

            run_batches(pool, gather_batch)

            for p, ps in enumerate(PASS):
                if ps["gather"] is None:
                    continue
                pool.wait_ge(table_ready, p)

                def gather(g, u, n, p=p, ps=ps):
                    pool.wait_ge(rec_in[u], rec_count(p, u, n))
                    pool.sem_inc(gat_started, 1)
                    for k in range(K):
                        pool.indirect_dma_start(G[:, u, k, :], None, ps["gather"], bass.IndirectOffsetOnAxis(
                            ap=wrec[:, u, k, 0:1], axis=0)).then_inc(G_in[u], 16)

                run_steps(pool, [(0, gather)])

        @block.scalar
        def _(act):
            def square(b, par, n):
                act.wait_ge(attr_in[par], n * 32 + 32)
                if not early(b, 2):
                    act.wait_ge(sum_used, b - 1)
                nc.scalar.activation(prod2[:, par, :], attr[:, par, :], ACT.Square).then_inc(attr_sq, 1)

            run_batches(act, square)
            act.wait_ge(sums_done, 1)
            nc.scalar.activation(nrm[:, :], ssq[:, :], ACT.Sqrt)
            nc.scalar.activation(qn[:, 1:2], qn[:, 0:1], ACT.Sqrt).then_inc(roots_done, 1)
            act.wait_ge(wsT_done, 1)
            nc.scalar.activation(w_selfT[:, :], bank[1][:, 0:D], ACT.Copy).then_inc(wsT_copied, 1)

            def msg_copy(n, c2):
                act.wait_ge(msg_T, n + 1)
                nc.scalar.activation(gatT[:, c2, :], bank[0][:, 0:EP], ACT.Copy)
                nc.scalar.activation(rohT[:, c2, :], bank[0][0:R, P:P + EP], ACT.Copy).then_inc(msg_Tc, 1)

            def msg_pick(n, c2, par, c):
                act.wait_ge(msg_Z, n + 1)
                if not early(n, 2):
                    act.wait_ge(msg_sum, n - 1)
                lo, hi = REL_CUT[2]
                for r_ in range(lo, hi):
                    nc.scalar.activation(sel[:, c2, r_, :], bank[3 + 3 * c2][0:EP, (r_ - lo) * D:(r_ - lo + 1) * D],
                                         ACT.Copy, scale=roh[:, par, c, r_:r_ + 1])
                nc.scalar.activation(sel[:, c2, R, :], bank[7][0:EP, 0:D], ACT.Copy).then_inc(msg_act, 1)

            def msg_steps(b, par, nb_):
                for c in range(EB):
                    msg_copy(b * EB + c, c % 2)
                    if not (early(b, 1) and c == 0):
                        msg_pick(b * EB + (c - 1), (c - 1) % 2, par if c else 1 - par, (c - 1) % EB)

            run_batches(act, msg_steps)
            msg_pick(EC - 1, (EC - 1) % 2, (NB - 1) % 2, EB - 1)

            def sd(p):
                def stage(g, u, n):
                    act.wait_ge(var_done.sem, var_done.at(p, g))
                    nc.scalar.activation(sdb[:, u % 4, :], mvb[:, u % 4, :, 1], ACT.Sqrt, bias=eps_col[:, 0:1]).then_inc(sd_done.sem, 1)
                return stage

            def normed(p):
                def stage(g, u, n):
                    act.wait_ge(nb_done.sem, nb_done.at(p, g))
                    if not (p == 0 and early(g, 4)):
                        act.wait_ge(stored[u % 4], stored_before(p, u, n))
                    for j in range(J):
                        ins = nc.scalar.activation(o[:, u % 4, j, :], r[:, u % 4, j, :], ACT.Identity,
                                                   scale=rsb[:, u % 4, j:j + 1], bias=nbb[:, u % 4, j:j + 1])
                    ins.then_inc(o_done.sem, 1)
                return stage

            def copy_T(p, first_bank):
                def stage(g, u, n):
                    act.wait_ge(T_done.sem, T_done.at(p, g))
                    nc.scalar.activation(flat(yT, u % 4), bank[first_bank + u % 2][:, 0:J * D], ACT.Copy).then_inc(Tc_done.sem, 1)
                return stage

            def sd0(g, u, n):
                act.wait_ge(var0_done.sem, var0_done.at(0, g))
                nc.scalar.activation(sda[:, u % 4, :], mva[:, u % 4, :, 1], ACT.Sqrt, bias=eps_col[:, 0:1]).then_inc(sd0_done.sem, 1)

            def normed0(g, u, n):
                act.wait_ge(nb0_done.sem, nb0_done.at(0, g))
                for j in range(J):
                    ins = nc.scalar.activation(hx[:, u % 4, j, :], bj(2 + u % 4)[:, j, :], ACT.Identity,
                                               scale=rsa[:, u % 4, j:j + 1], bias=nba[:, u % 4, j:j + 1])
                ins.then_inc(n0_done.sem, 1)

            run_steps(act, [(1, copy_T(0, 0)), (3, sd0), (4, normed0), (5, sd(0)), (6, normed(0))])
            run_steps(act, [(2, copy_T(1, 2)), (4, sd(1)), (5, normed(1))])

            def gT_copy(g, u, n):
                act.wait_ge(T_done.sem, T_done.at(2, g))
                nc.scalar.activation(flat(gT, u % 4), bank[0][:, 0:GE], ACT.Copy).then_inc(Tc_done.sem, 1)

            def xdT_copy(g, u, n):
                act.wait_ge(xd_done.sem, xd_done.at(2, g))
                nc.scalar.activation(flat(xdT, u % 4), bank[3][:, 0:GE], ACT.Copy).then_inc(xdc_done.sem, 1)

            def gelu(g, u, n):
                act.wait_ge(hp_done.sem, hp_done.at(2, g))
                nc.scalar.activation(flat(hh, u % 4), bank[4][0:H, 0:GE], ACT.Gelu, bias=mb1[:, 0:1]).then_inc(hh_done.sem, 1)

            def edge_tanh(g, u, n):
                act.wait_ge(ep_done.sem, ep_done.at(2, g))
                nc.scalar.activation(th[:, u % 4, :], bank[5][:, 0:K], ACT.Tanh, scale=0.5, bias=mb2h[:, 0:1]).then_inc(th_done.sem, 1)

            def scaled_rows(g, u, n):
                act.wait_ge(di_done.sem, di_done.at(2, g))
                act.wait_ge(stored[u % 4], stored_before(2, u, n))
                for j in range(J):
                    ins = nc.scalar.activation(o[:, u % 4, j, :], xa[:, u, j, :], ACT.Copy, scale=ny[:, u % 2, j:j + 1])
                ins.then_inc(o_done.sem, 1)

            run_steps(act, [(1, gT_copy), (2, xdT_copy), (3, gelu), (4, edge_tanh), (7, scaled_rows)])
            run_steps(act, [(2, copy_T(3, 2)), (4, sd(3)), (5, normed(3))])

            def half(g, u, n):
                act.wait_ge(xa_in[u], xa_count(4, u, n))
                if not early(g, 4):
                    act.wait_ge(o_done.sem, o_done.at(4, g - 4))
                nc.scalar.activation(flat(hx, u % 4), flat(xa, u), ACT.Copy, scale=0.5).then_inc(half_done.sem, 1)

            run_steps(act, [(1, half)])
            run_steps(act, [(3, sd(5)), (4, normed(5))])

        @block.vector
        def _(dve):
            chain = [0]

            def link(ins):
                chain[0] += 1
                ins.then_inc(dve_own, 1)
                dve.wait_ge(dve_own, chain[0])

            dve.wait_ge(edges_in, 48)
            nc.vector.tensor_copy(dstf[:, :], dst_n[:, :])
            link(nc.vector.tensor_copy(typf[:, :], typ_n[:, :]))
            dve.wait_ge(consts, 2)
            nc.vector.tensor_tensor(out=rel_1h[:, :, :], in0=typf[:, :].unsqueeze(2).to_broadcast((EP, EC, R)),
                                    in1=rel_iota[0:EP, :].unsqueeze(1).to_broadcast((EP, EC, R)), op=ALU.is_equal)
            for b0 in range(0, NG, CB):
                w = min(CB, NG - b0)
                link(nc.vector.tensor_tensor(out=cmp_t[:, 0:w, :], in0=dstf[:, :].unsqueeze(1).to_broadcast((EP, w, EC)),
                                             in1=group_base[0:EP, b0:b0 + w].unsqueeze(2).to_broadcast((EP, w, EC)), op=ALU.is_lt))
                link(nc.vector.tensor_reduce(out=cnt[:, b0:b0 + w], in_=cmp_t[:, 0:w, :], axis=AX.X, op=ALU.add))
            dve.sem_inc(cnt_done, 1)
            dve.wait_ge(e0_sum, 1)
            nc.vector.tensor_copy(e0_row[:, :], bank[0][0:1, 0:NG]).then_inc(e0_ready, 1)

            dve.wait_ge(weights_in, 16 * NW)
            nc.vector.tensor_scalar(mb2h[:, :], mb2[:, :], 0.5, None, ALU.mult)
            link(nc.vector.tensor_tensor(out=qsq[:, :], in0=qb[:, :], in1=qb[:, :], op=ALU.mult))
            link(nc.vector.tensor_reduce(out=qn[:, 0:1], in_=qsq[:, :], axis=AX.X, op=ALU.add))

            def attr_batch(b, par, n):
                dve.wait_ge(attr_in[par], n * 32 + 32)
                nc.vector.tensor_tensor(out=prod[:, par, :].rearrange("p (c d) -> p c d", d=D),
                                        in0=attr[:, par, :].rearrange("p (c d) -> p c d", d=D),
                                        in1=qb[0:EP, :].unsqueeze(1).to_broadcast((EP, EB, D)), op=ALU.mult).then_inc(attr_mul, 1)
                dve.wait_ge(attr_sq, b + 1)
                nc.vector.tensor_reduce(out=ssq[:, cut(b, EB)], in_=prod2[:, par, :].rearrange("p (c d) -> p c d", d=D),
                                        axis=AX.X, op=ALU.add).then_inc(sum_used, 1)
                dve.wait_ge(attr_mul, b + 1)
                nc.vector.tensor_reduce(out=dotq[:, cut(b, EB)], in_=prod[:, par, :].rearrange("p (c d) -> p c d", d=D), axis=AX.X, op=ALU.add)

            run_batches(dve, attr_batch)
            link(nc.vector.tensor_copy(qn[:, 3:4], qn[:, 0:1]))
            dve.sem_inc(sums_done, 1)
            dve.wait_ge(roots_done, 1)
            nc.vector.tensor_scalar(nrm[:, :], nrm[:, :], EPS_Q, None, ALU.max)
            link(nc.vector.tensor_scalar(qn[:, 1:2], qn[:, 1:2], EPS_Q, None, ALU.max))
            nc.vector.reciprocal(nrm[:, :], nrm[:, :])
            link(nc.vector.reciprocal(qn[:, 2:3], qn[:, 1:2]))
            link(nc.vector.tensor_scalar(dotq[:, :], dotq[:, :], qn[0:EP, 2:3], None, ALU.mult))
            dve.wait_ge(consts, 2)
            nc.vector.tensor_copy(rec_n[:, :, 0], src_n[:, :])
            nc.vector.tensor_copy(rec_n[:, :, 1].bitcast(f32), dstf[:, :])
            nc.vector.tensor_tensor(out=rec_n[:, :, 2].bitcast(f32), in0=dotq[:, :], in1=nrm[:, :], op=ALU.mult).then_inc(rec_done, 1)

            def msg_steps(b, par, nb_):
                if not (isinstance(b, int) and b == NB - 1):
                    nc.vector.tensor_copy(roh[:, 1 - par, :, :], rel_1h[:, cut(b + 1, EB), :]).then_inc(roh_ready, 1)
                dve.wait_ge(roh_ready, b + 1)
                if not early(b, 2):
                    dve.wait_ge(msg_out[par], nb_ * 16)
                for c in range(EB):
                    n, c2 = b * EB + c, c % 2
                    dve.wait_ge(msg_Z, n + 1)
                    for q, (lo, hi) in enumerate(REL_CUT[:2]):
                        ins = nc.vector.tensor_tensor(
                            out=sel[:, c2, lo:hi, :], in0=bank[1 + q + 3 * c2][0:EP, 0:(hi - lo) * D].rearrange("p (r d) -> p r d", d=D),
                            in1=roh[:, par, c, lo:hi].unsqueeze(2).to_broadcast((EP, hi - lo, D)), op=ALU.mult)
                    ins.then_inc(msg_sel, 1)
                    dve.wait_ge(msg_sel, n + 1)
                    dve.wait_ge(msg_act, n + 1)
                    nc.vector.tensor_reduce(out=msum[:, par, c, :], in_=sel[:, c2, :, :].rearrange("p r d -> p d r"),
                                            axis=AX.X, op=ALU.add).then_inc(msg_sum, 1)

            nc.vector.tensor_copy(roh[:, 0, :, :], rel_1h[:, 0:EB, :]).then_inc(roh_ready, 1)
            run_batches(dve, msg_steps)

            def drel_of(p):
                def stage(g, u, n):
                    dve.wait_ge(rec_in[u], rec_count(p, u, n))
                    nc.vector.tensor_scalar(drel[:, u, :], wrec[:, u, :, 1].bitcast(f32), group_base[:, cut(g, 1)],
                                            None, ALU.subtract).then_inc(drel_done.sem, 1)
                return stage

            def S_of(p, weight):
                def stage(g, u, n):
                    dve.wait_ge(drel_done.sem, drel_done.at(p, g))
                    for k in range(K):
                        if weight is None:
                            w, op = None, ALU.bypass
                        elif weight == "sim":
                            w, op = wrec[:, u, k, 2:3].bitcast(f32), ALU.mult
                        else:
                            w, op = cell(ew_tab, g, k), ALU.mult
                        ins = nc.vector.tensor_scalar(S[:, u, k, :, :], node_iota[:, :, :], drel[:, u, k:k + 1], w, ALU.is_equal, op)
                    ins.then_inc(S_done.sem, 1)
                return stage

            def variance(src3, st, m, u4, p, g, bn, var):
                for j in range(J):
                    ins = nc.vector.bn_stats(st[:, u4, j, :], src3[:, j, :])
                ins.then_inc(bn.sem, 1)
                dve.wait_ge(bn.sem, bn.at(p, g))
                dve.sem_inc(aggr_started, 1)
                for j in range(J):
                    ins = nc.vector.bn_aggr(m[:, u4, j, :], st[:, u4, j, :])
                ins.then_inc(var.sem, 1)

            def inverse(p, sdt, rst, nbt, m, sd_, rs_, nb_):
                def stage(g, u, n):
                    dve.wait_ge(sd_.sem, sd_.at(p, g))
                    nc.vector.reciprocal(rst[:, u % 4, :], sdt[:, u % 4, :]).then_inc(rs_.sem, 1)
                    dve.wait_ge(rs_.sem, rs_.at(p, g))
                    nc.vector.scalar_tensor_tensor(out=nbt[:, u % 4, :], in0=m[:, u % 4, :, 0], scalar=-1.0, in1=rst[:, u % 4, :],
                                                   op0=ALU.mult, op1=ALU.mult).then_inc(nb_.sem, 1)
                return stage

            def inverse_out(p):
                return inverse(p, sdb, rsb, nbb, mvb, sd_done, rs_done, nb_done)

            def variance_out(p, g, u):
                variance(r[:, u % 4, :, :], st6b, mvb, u % 4, p, g, bn_done, var_done)

            def var0(g, u, n):
                dve.wait_ge(H_done.sem, H_done.at(0, g))
                variance(bj(2 + u % 4), st6a, mva, u % 4, 0, g, bn0_done, var0_done)

            def mid(g, u, n):
                dve.wait_ge(n0_done.sem, n0_done.at(0, g))
                r_u = r[:, u % 4, :, :]
                nc.vector.tensor_tensor(out=r_u, in0=hx[:, u % 4, :, :], in1=gam[:, :].unsqueeze(1).to_broadcast((P, J, D)), op=ALU.mult).then_inc(mid_done.sem, 1)
                dve.wait_ge(mid_done.sem, mid_done.at(0, g, 1))
                nc.vector.tensor_tensor(out=r_u, in0=r_u, in1=bet[:, :].unsqueeze(1).to_broadcast((P, J, D)), op=ALU.add).then_inc(mid_done.sem, 1)
                dve.wait_ge(mid_done.sem, mid_done.at(0, g, 2))
                nc.vector.tensor_tensor(out=r_u, in0=r_u, in1=xa[:, u, :, :], op=ALU.add).then_inc(mid_done.sem, 1)
                dve.wait_ge(mid_done.sem, mid_done.at(0, g, 3))
                variance_out(0, g, u)

            run_steps(dve, [(0, drel_of(0)), (1, S_of(0, None)), (3, var0),
                            (4, inverse(0, sda, rsa, nba, mva, sd0_done, rs0_done, nb0_done)), (5, mid), (6, inverse_out(0))])

            def y_of(p):
                def stage(g, u, n):
                    dve.wait_ge(agg_done.sem, agg_done.at(p, g))
                    dve.wait_ge(xa_in[u], xa_count(p, u, n))
                    nc.vector.tensor_tensor(out=y[:, u % 4, :, :], in0=bj(u % 2), in1=xa[:, u, :, :], op=ALU.add).then_inc(y_done.sem, 1)
                return stage

            def relu_sum(g, u, n):
                dve.wait_ge(H_done.sem, H_done.at(1, g))
                nc.vector.scalar_tensor_tensor(out=flat(r, u % 4), in0=bank[4 + u % 2][:, 0:J * D], scalar=0.0,
                                               in1=flat(xa, u), op0=ALU.max, op1=ALU.add).then_inc(sum_done.sem, 1)
                dve.wait_ge(sum_done.sem, sum_done.at(1, g))
                variance_out(1, g, u)

            run_steps(dve, [(0, drel_of(1)), (1, S_of(1, None)), (2, y_of(1)), (4, relu_sum), (5, inverse_out(1))])

            def sT_copy(g, u, n):
                dve.wait_ge(T_done.sem, T_done.at(2, g))
                if not early(g, 2):
                    dve.wait_ge(xd_done.sem, xd_done.at(2, g - 2))
                for k in range(K):
                    ins = nc.vector.tensor_copy(sT[:, u % 2, k, :, :].rearrange("p j e -> p (j e)"), bank[1 + k][:, 0:J * P])
                ins.then_inc(sTc_done.sem, 1)

            def edge_weight(g, u, n):
                dve.wait_ge(th_done.sem, th_done.at(2, g))
                nc.vector.tensor_scalar(ew1[:, u % 4, :, 0], th[:, u % 4, :], 0.5, 0.5, ALU.mult, ALU.add)
                nc.vector.tensor_scalar(col(ew_tab, g), th[:, u % 4, :], 0.5, 0.5, ALU.mult, ALU.add).then_inc(ew_done.sem, 1)

            def degrees(g, u, n):
                u2, k = u % 2, [0]

                def then(ins):
                    k[0] += 1
                    ins.then_inc(di_done.sem, 1)
                    if k[0] < di_done.per:
                        dve.wait_ge(di_done.sem, di_done.at(2, g, k[0]))

                sums = bank[6][:, 0:2 * J].rearrange("p (j t) -> p j t", t=2)
                dve.wait_ge(dg_done.sem, dg_done.at(2, g))
                if not early(g, 2):
                    dve.wait_ge(o_done.sem, o_done.at(2, g - 2))
                then(nc.vector.tensor_scalar(nd[:, u2, :], sums[:, :, 0], 1.0, None, ALU.add))
                then(nc.vector.tensor_scalar(dg[:, u2, :, 0], sums[:, :, 1], 1.0, None, ALU.max))
                then(nc.vector.reciprocal(dg[:, u2, :, 1], dg[:, u2, :, 0]))
                then(nc.vector.tensor_scalar(col(chalf_tab, g), dg[:, u2, :, 1], 0.5, None, ALU.mult))
                y_u, d_u, a_u = ny[:, u2, :], nd[:, u2, :], na[:, u2, :]
                then(nc.vector.tensor_scalar(a_u.bitcast(i32), d_u.bitcast(i32), 1, None, ALU.arith_shift_right))
                then(nc.vector.tensor_scalar(y_u.bitcast(i32), a_u.bitcast(i32), -1.0, float(0x5f3759df), ALU.mult, ALU.add))
                for _ in range(NEWTON):
                    then(nc.vector.tensor_tensor(out=a_u, in0=y_u, in1=y_u, op=ALU.mult))
                    then(nc.vector.scalar_tensor_tensor(out=a_u, in0=a_u, scalar=-0.5, in1=d_u, op0=ALU.mult, op1=ALU.mult))
                    then(nc.vector.scalar_tensor_tensor(out=y_u, in0=a_u, scalar=1.5, in1=y_u, op0=ALU.add, op1=ALU.mult))
                then(nc.vector.tensor_copy(col(dinv_tab, g), y_u))
                assert k[0] == di_done.per

            run_steps(dve, [(0, drel_of(2)), (1, S_of(2, None)), (1, sT_copy), (5, edge_weight), (7, degrees)])

            def conv_sum(g, u, n):
                dve.wait_ge(xb_in[u], xb_count(3, u, n))
                nc.vector.tensor_tensor(out=hx[:, u % 4, :, :], in0=xb[:, u, :, :], in1=cb[:, :].unsqueeze(1).to_broadcast((P, J, D)),
                                        op=ALU.add).then_inc(base_done.sem, 1)
                dve.wait_ge(base_done.sem, base_done.at(3, g))
                dve.wait_ge(H_done.sem, H_done.at(3, g))
                for j in range(J):
                    ins = nc.vector.scalar_tensor_tensor(out=r[:, u % 4, j, :], in0=bj(4 + u % 2)[:, j, :], scalar=cell(dinv_tab, g, j),
                                                         in1=hx[:, u % 4, j, :], op0=ALU.mult, op1=ALU.add)
                ins.then_inc(sum_done.sem, 1)
                dve.wait_ge(sum_done.sem, sum_done.at(3, g))
                variance_out(3, g, u)

            run_steps(dve, [(0, drel_of(3)), (1, S_of(3, "ew")), (2, y_of(3)), (4, conv_sum), (5, inverse_out(3))])

            def h1_of(g, u, n):
                dve.wait_ge(agg_done.sem, agg_done.at(4, g))
                dve.wait_ge(half_done.sem, half_done.at(4, g))
                dve.wait_ge(stored[u % 4], stored_before(4, u, n))
                for j in range(J):
                    ins = nc.vector.scalar_tensor_tensor(out=o[:, u % 4, j, :], in0=bj(u % 2)[:, j, :], scalar=cell(chalf_tab, g, j),
                                                         in1=hx[:, u % 4, j, :], op0=ALU.mult, op1=ALU.add)
                ins.then_inc(o_done.sem, 1)

            run_steps(dve, [(0, drel_of(4)), (1, S_of(4, "sim")), (2, h1_of)])

            def h2_sum(g, u, n):
                dve.wait_ge(xa_in[u], xa_count(5, u, n))
                dve.wait_ge(xb_in[u], xb_count(5, u, n))
                nc.vector.scalar_tensor_tensor(out=flat(hx, u % 4), in0=flat(xa, u), scalar=0.5, in1=flat(xb, u),
                                               op0=ALU.mult, op1=ALU.add).then_inc(base_done.sem, 1)
                dve.wait_ge(base_done.sem, base_done.at(5, g))
                dve.wait_ge(agg_done.sem, agg_done.at(5, g))
                for j in range(J):
                    ins = nc.vector.scalar_tensor_tensor(out=r[:, u % 4, j, :], in0=bj(u % 2)[:, j, :], scalar=cell(chalf_tab, g, j),
                                                         in1=hx[:, u % 4, j, :], op0=ALU.mult, op1=ALU.add)
                ins.then_inc(sum_done.sem, 1)
                dve.wait_ge(sum_done.sem, sum_done.at(5, g))
                variance_out(5, g, u)

            run_steps(dve, [(0, drel_of(5)), (1, S_of(5, "sim")), (3, h2_sum), (4, inverse_out(5))])

        @block.tensor
        def _(pe):
            pe.wait_ge(consts, 3)
            pe.wait_ge(cnt_done, 1)
            nc.tensor.matmul(bank[0][0:1, 0:NG], ones_col[0:EP, :], cnt[:, :], start=True, stop=True).then_inc(e0_sum, 1)
            pe.wait_ge(weights_in, 16 * NW)
            nc.tensor.transpose(bank[1][:, 0:D], w_raw[:, :], ident[:, :]).then_inc(wsT_done, 1)
            pe.wait_ge(wsT_copied, 1)
            pe.wait_ge(e0_ready, 1)

            def msg_T_of(n, c, par, b):
                pe.wait_ge(gat_in[c % 4], b * (16 * EB // 4) + 16 * (c // 4 + 1))
                if c == 0:
                    pe.wait_ge(roh_ready, b + 1)
                if not early(n, 1):
                    pe.wait_ge(msg_Tc, n)
                nc.tensor.transpose(bank[0][:, 0:EP], gat[:, c % 4, :], ident[0:EP, 0:EP])
                nc.tensor.transpose(bank[0][0:R, P:P + EP], roh[:, par, c, :], ident[0:EP, 0:EP]).then_inc(msg_T, 1)

            def msg_Z_of(n, c2):
                pe.wait_ge(msg_Tc, n + 1)
                if not early(n, 2):
                    pe.wait_ge(msg_sel, n - 1)
                if not early(n, 1):
                    pe.wait_ge(msg_act, n)
                for q, (lo, hi) in enumerate(REL_CUT):
                    nc.tensor.matmul(bank[1 + q + 3 * c2][0:EP, 0:(hi - lo) * D], gatT[:, c2, :], w_rel[:, lo * D:hi * D], start=True, stop=True)
                nc.tensor.matmul(bank[7][0:EP, 0:D], rohT[:, c2, :], b_rel[:, :], start=True, stop=True).then_inc(msg_Z, 1)

            def msg_steps(b, par, nb_):
                for c in range(EB):
                    msg_T_of(b * EB + c, c, par, b)
                    if not (early(b, 1) and c == 0):
                        msg_Z_of(b * EB + (c - 1), (c - 1) % 2)

            run_batches(pe, msg_steps)
            msg_Z_of(EC - 1, (EC - 1) % 2)

            def sums(p, first):
                def stage(g, u, n):
                    pe.wait_ge(S_done.sem, S_done.at(p, g))
                    pe.wait_ge(G_in[u], G_count(p, u, n))
                    free = {1: y_done, 3: y_done, 4: o_done, 5: sum_done}[p]
                    if not early(g, 2):
                        pe.wait_ge(free.sem, free.at(p, g - 2))
                    for j in range(J):
                        for k in range(K):
                            ins = nc.tensor.matmul(bj(u % 2)[:, j, :], S[:, u, k, j, :], G[:, u, k, :], start=(k == 0), stop=(k == K - 1))
                    ins.then_inc(agg_done.sem, 1)
                return stage

            def flip(p, first):
                def stage(g, u, n):
                    if p == 0:
                        pe.wait_ge(xa_in[u], xa_count(p, u, n))
                    else:
                        pe.wait_ge(y_done.sem, y_done.at(p, g))
                    if not early(g, 2):
                        pe.wait_ge(Tc_done.sem, Tc_done.at(p, g - 2))
                    for j in range(J):
                        rows = xa[:, u, j, :] if p == 0 else y[:, u % 4, j, :]
                        ins = nc.tensor.transpose(bj(first + u % 2)[:, j, :], rows, ident[:, :])
                    ins.then_inc(T_done.sem, 1)
                return stage

            def self_and_messages(g, u, n):
                pe.wait_ge(Tc_done.sem, Tc_done.at(0, g))
                pe.wait_ge(S_done.sem, S_done.at(0, g))
                pe.wait_ge(M_in[u], n * 16 + 16)
                if not early(g, 4):
                    pe.wait_ge(n0_done.sem, n0_done.at(0, g - 4))
                b_ = bank[2 + u % 4][:, 0:J * D]
                nc.tensor.matmul(b_, ones_row[:, :], b_self_row[0:1, :, :].rearrange("a j d -> a (j d)"), start=True, stop=False)
                for j in range(J):
                    nc.tensor.matmul(bj(2 + u % 4)[:, j, :], yT[:, u % 4, j, :], w_selfT[:, :], start=False, stop=False)
                    for k in range(K):
                        ins = nc.tensor.matmul(bj(2 + u % 4)[:, j, :], S[:, u, k, j, :], G[:, u, k, :], start=False, stop=(j == J - 1 and k == K - 1))
                ins.then_inc(H_done.sem, 1)

            run_steps(pe, [(1, flip(0, 0)), (2, self_and_messages)])

            def weighted(p, w_t, bias):
                def stage(g, u, n):
                    pe.wait_ge(Tc_done.sem, Tc_done.at(p, g))
                    if not early(g, 2):
                        pe.wait_ge(sum_done.sem, sum_done.at(p, g - 2))
                    b_ = bank[4 + u % 2][:, 0:J * D]
                    if bias is not None:
                        nc.tensor.matmul(b_, ones_row[:, :], bias[0:1, :, :].rearrange("a j d -> a (j d)"), start=True, stop=False)
                    for j in range(J):
                        ins = nc.tensor.matmul(bj(4 + u % 2)[:, j, :], yT[:, u % 4, j, :], w_t[:, :], start=bias is None,
                                               stop=bias is None or j == J - 1)
                    ins.then_inc(H_done.sem, 1)
                return stage

            run_steps(pe, [(2, flip(1, 2)), (1, sums(1, 0)), (3, weighted(1, w1_sb, b1_row))])

            def flips(g, u, n):
                pe.wait_ge(S_done.sem, S_done.at(2, g))
                pe.wait_ge(G_in[u], G_count(2, u, n))
                if not early(g, 1):
                    pe.wait_ge(Tc_done.sem, Tc_done.at(2, g - 1))
                    pe.wait_ge(sTc_done.sem, sTc_done.at(2, g - 1))
                for k in range(K):
                    nc.tensor.transpose(bank[0][:, k * P:(k + 1) * P], G[:, u, k, :], ident[:, :])
                    for j in range(J):
                        ins = nc.tensor.transpose(bank[1 + k][:, j * P:(j + 1) * P], S[:, u, k, j, :], ident[:, :])
                ins.then_inc(T_done.sem, 1)

            def dst_rows(g, u, n):
                pe.wait_ge(sTc_done.sem, sTc_done.at(2, g))
                pe.wait_ge(xa_in[u], xa_count(2, u, n))
                if not early(g, 1):
                    pe.wait_ge(xdc_done.sem, xdc_done.at(2, g - 1))
                for j in range(J):
                    ins = nc.tensor.matmul(bank[3][:, 0:GE].rearrange("p (k e) -> p k e", k=K), xa[:, u, j, :], sT[:, u % 2, :, j, :], start=(j == 0), stop=(j == J - 1))
                ins.then_inc(xd_done.sem, 1)

            def hidden(g, u, n):
                pe.wait_ge(Tc_done.sem, Tc_done.at(2, g))
                pe.wait_ge(xdc_done.sem, xdc_done.at(2, g))
                if not early(g, 1):
                    pe.wait_ge(hh_done.sem, hh_done.at(2, g - 1))
                nc.tensor.matmul(bank[4][0:H, 0:GE], mw1[:, 0, :], flat(gT, u % 4), start=True, stop=False)
                nc.tensor.matmul(bank[4][0:H, 0:GE], mw1[:, 1, :], flat(xdT, u % 4), start=False, stop=True).then_inc(hp_done.sem, 1)

            def logits(g, u, n):
                pe.wait_ge(hh_done.sem, hh_done.at(2, g))
                if not early(g, 1):
                    pe.wait_ge(th_done.sem, th_done.at(2, g - 1))
                for k in range(K):
                    ins = nc.tensor.matmul(bank[5][:, k:k + 1], hh[:, u % 4, k, :], mw2[:, :], start=True, stop=True)
                ins.then_inc(ep_done.sem, 1)

            def degree_sums(g, u, n):
                pe.wait_ge(ew_done.sem, ew_done.at(2, g))
                if not early(g, 1):
                    pe.wait_ge(di_done.sem, di_done.at(2, g - 1, 2))
                for j in range(J):
                    for k in range(K):
                        ins = nc.tensor.matmul(bank[6][:, 2 * j:2 * j + 2], S[:, u, k, j, :], ew1[:, u % 4, k, :], start=(k == 0), stop=(k == K - 1))
                ins.then_inc(dg_done.sem, 1)

            run_steps(pe, [(1, flips), (2, dst_rows), (3, hidden), (4, logits), (6, degree_sums)])

            run_steps(pe, [(2, flip(3, 2)), (1, sums(3, 0)), (3, weighted(3, cw, None))])
            run_steps(pe, [(1, sums(4, 0))])
            run_steps(pe, [(1, sums(5, 0))])


_INS = ["x", "src", "dst", "edge_attr_128", "edge_type_10", "L0_gnn_relation_weights", "L0_gnn_relation_bias",
        "L0_gnn_w_self", "L0_gnn_b_self", "L0_gnn_ln_gamma", "L0_gnn_ln_beta", "L1_gnn_W", "L1_gnn_b",
        "L2_gnn_mlp_w1", "L2_gnn_mlp_b1", "L2_gnn_mlp_w2", "L2_gnn_mlp_b2", "L2_gnn_conv_w", "L2_gnn_conv_b",
        "L3_gnn_question_emb"]


def kernel(**inputs):
    import numpy as _np
    import concourse.bacc as _bacc
    from concourse import mybir as _mybir
    from concourse.bass_utils import run_bass_kernel_spmd as _run

    nc = _bacc.Bacc("TRN2", target_bir_lowering=False, num_devices=1)
    arrays, args = {}, []
    for name in _INS:
        a = _np.ascontiguousarray(inputs[name])
        arrays[f"in_{name}_dram"] = a
        args.append(nc.dram_tensor(f"in_{name}_dram", a.shape, _mybir.dt.from_np(a.dtype), kind="ExternalInput").ap())
    shape = _np.asarray(inputs["x"]).shape
    args.append(nc.dram_tensor("out_0_dram", shape, _mybir.dt.float32, kind="ExternalOutput").ap())
    gnn_kernel(nc, *args)
    r = _run(nc, [arrays], core_ids=[0])
    return r.results[0]["out_0_dram"]
```

```python
import concourse.bass as bass
from concourse import mybir
from contextlib import ExitStack


def gnn_kernel(nc, x, src, dst, edge_attr, edge_type, rel_w, rel_b, w_self, b_self, ln_g, ln_b,
               w1, b1, mlp_w1, mlp_b1, mlp_w2, mlp_b2, conv_w, conv_b, q_emb, out):
    f32, i32, bf16 = mybir.dt.float32, mybir.dt.int32, mybir.dt.bfloat16
    ALU, ACT, AX = mybir.AluOpType, mybir.ActivationFunctionType, mybir.AxisListType
    N, D = x.shape
    E = src.shape[0]
    R = rel_w.shape[0]
    H = mlp_w1.shape[1]
    P, J, K = 128, 3, 2
    GN, GE = P * J, P * K
    NG = -(-N // GN)
    NPAD = NG * GN
    RING = 8
    LAST = N - (NG - 1) * GN
    EP, EC, EB = 125, E // 125, 8
    NB = EC // EB
    REL_CUT = ((0, 4), (4, 8), (8, R))
    PARTS = 3
    NW = 16
    EPS_LN, EPS_Q = 1e-5, 1e-12

    ctx = ExitStack()
    with ctx:
        def sb(name, shape, dt=f32):
            return ctx.enter_context(nc.sbuf_tensor(name, shape, dt))

        def sem(name):
            return ctx.enter_context(nc.semaphore(name))

        def dram(name, rows, cols, dt=f32):
            return nc.dram_tensor(name, (rows, cols), dt, kind="Internal").ap()

        msg0 = dram("msg0", E + GE, D)
        rec = dram("rec", E + GE, 4, i32)
        dst_parts = dram("dst_parts", 2, E + GE, bf16)
        bias_parts = dram("bias_parts", PARTS, 3 * D, bf16)
        x1 = dram("x1", NPAD, D)
        x2 = dram("x2", NPAD, D)
        x2s = dram("x2s", NPAD, D)
        x3 = dram("x3", NPAD, D)
        h1 = dram("h1", NPAD, D)
        extra = dram("extra", NPAD + P, D)
        node_num = dram("node_num", NPAD, 2)

        ident = sb("ident", [P, P])
        half_ident = sb("half_ident", [P, P])
        node_iota = sb("node_iota", [P, J, P])
        group_base = sb("group_base", [P, NG])
        rel_iota = sb("rel_iota", [P, R])
        ones_row = sb("ones_row", [1, P])
        ones_col = sb("ones_col", [P, 1])
        eps_col = sb("eps_col", [P, 1])
        zero_pad = sb("zero_pad", [P, K * D])
        rec_pad = sb("rec_pad", [P, K, 4], i32)
        w_rel = sb("w_rel", [D, R * D])
        b_rel = sb("b_rel", [R, D])
        w_raw = sb("w_raw", [D, D])
        w_selfT = sb("w_selfT", [D, D])
        bias16 = sb("bias16", [PARTS, 3, J, D], bf16)
        ones16 = sb("ones16", [PARTS, P], bf16)
        gam = sb("gam", [P, D])
        bet = sb("bet", [P, D])
        w1_sb = sb("w1_sb", [D, D])
        mw1 = sb("mw1", [D, 2, H])
        mb1 = sb("mb1", [H, 1])
        mw2 = sb("mw2", [H, 1])
        mb2 = sb("mb2", [P, 1])
        mb2h = sb("mb2h", [P, 1])
        cw = sb("cw", [D, D])
        qb = sb("qb", [P, D])
        qsq = sb("qsq", [P, D])
        qn = sb("qn", [P, 4])

        src_n = sb("src_n", [EP, EC], i32)
        dst_n = sb("dst_n", [EP, EC], i32)
        typ_n = sb("typ_n", [EP, EC], i32)
        dstf = sb("dstf", [EP, EC])
        typf = sb("typf", [EP, EC])
        dotq = sb("dotq", [EP, EC])
        ssq = sb("ssq", [EP, EC])
        rec_n = sb("rec_n", [EP, EC, 4], i32)
        rel_1h = sb("rel_1h", [EP, EC, R])
        CB = 11
        picks = sb("picks", [EP, 2 * (R + 1) * D])
        cmp_t = picks[:, 0:CB * EC].rearrange("p (b c) -> p b c", b=CB)
        sel = picks[:, :].rearrange("p (c r d) -> p c r d", c=2, r=R + 1)
        cnt = sb("cnt", [EP, NG + 1])
        e0_row = sb("e0_row", [1, NG], i32)
        attr = sb("attr", [EP, 2, EB * D])
        prod = sb("prod", [EP, 2, EB * D])
        prod2 = sb("prod2", [EP, 2, EB * D])
        nrm = sb("nrm", [EP, EC])
        next_n = sb("next_n", [EP, 1], i32)
        dst_hi = sb("dst_hi", [EP, EC], bf16)
        dst_lo = sb("dst_lo", [EP, EC], bf16)
        next_f = sb("next_f", [EP, 1])
        size_row = sb("size_row", [1, NG + 1])
        flag_f = sb("flag_f", [1, 2])
        flag_i = sb("flag_i", [1, 1], i32)
        flag_col = sb("flag_col", [EP, 1])
        ew_n, wc_n, ws_n = ssq, dotq, nrm
        own_dst = sb("own_dst", [EP, 1])
        row_f = sb("row_f", [EP, 4])
        trash_row = sb("trash_row", [EP, 1])
        row_i = sb("row_i", [EP, 1], i32)
        src_i = sb("src_i", [EP, 1], i32)
        dst_i = sb("dst_i", [EP, 1], i32)
        nums = sb("nums", [EP, 2])
        idx_b = sb("idx_b", [EP, 2, EB], i32)
        gat = sb("gat", [EP, 4, D])
        gatT = sb("gatT", [D, 2, EP])
        rohT = sb("rohT", [R, 2, EP])
        roh = sb("roh", [EP, 2, EB, R])
        msum = sb("msum", [EP, 2, EB, D])
        ones_sq, lower, same, diag_n = (picks[:, q * EP:(q + 1) * EP] for q in range(4))
        val, tot = picks[:, 4 * EP:4 * EP + D], picks[:, 4 * EP + D:4 * EP + 2 * D]
        rows_s, rows_d = gat[:, 0, :], gat[:, 1, :]

        xa = sb("xa", [P, RING, J, D])
        bias_f, bias_rest = xa[0:1, 0, :, :], xa[0:1, 1, :, :]
        bias_cut = (xa[0:1, 2:4, :, :].rearrange("a u j d -> a (u j d)").bitcast(bf16)[:, 0:PARTS * 3 * D]
                    .rearrange("a (t b d) -> a t b d", t=PARTS, b=3))
        dst_pad = xa[0:1, 4, :, :].rearrange("a j d -> a (j d)").bitcast(bf16)[:, 0:2 * GE].rearrange("a (t e) -> a t e", t=2)
        xb = sb("xb", [P, RING, J, D])
        wrec = sb("wrec", [P, RING, K, 4], i32)
        G = sb("G", [P, RING, K, D])
        S = sb("S", [P, RING, K, J, P])
        yT = sb("yT", [P, 4, J, D])
        r = sb("r", [P, 4, J, D])
        st6a = sb("st6a", [P, 4, J, 6])
        mva = sb("mva", [P, 4, J, 2])
        sda = sb("sda", [P, 4, J])
        rsa = sb("rsa", [P, 4, J])
        nba = sb("nba", [P, 4, J])
        st6b = sb("st6b", [P, 4, J, 6])
        mvb = sb("mvb", [P, 4, J, 2])
        sdb = sb("sdb", [P, 4, J])
        rsb = sb("rsb", [P, 4, J])
        nbb = sb("nbb", [P, 4, J])
        o = sb("o", [P, 4, J, D])
        hx = sb("hx", [P, 4, J, D])
        drel_tab = sb("drel_tab", [P, NG, K])
        sim_tab = sb("sim_tab", [P, NG, K])
        ew_tab = sb("ew_tab", [P, NG, K])
        simw_tab = sb("simw_tab", [P, NG, K])
        node16 = sb("node16", [P, NG, J, 2, PARTS], bf16)
        node_tab = sb("node_tab", [P, NG, J, 2])
        dinv2_tab = sb("dinv2_tab", [P, NG, J])
        gT = sb("gT", [D, 4, K, P])
        sT = sb("sT", [P, 2, J, GE])
        xdT = sb("xdT", [D, 2, GE])
        hh = sb("hh", [H, 4, K, P])
        th = sb("th", [P, 4, K])
        ew16 = sb("ew16", [P, 4, K, PARTS + 1], bf16)
        ew_rest = sb("ew_rest", [P, 4, K])
        drow = sb("drow", [2, RING, GE], bf16)
        node_id = sb("node_id", [P, NG, J])
        deg_tab = sb("deg_tab", [P, NG, J, 2])
        hx_all = hx[:, :, :, :].rearrange("p a j d -> p (a j d)")
        nt_y, nt_a, nt_d = (hx_all[:, q * NG * J:(q + 1) * NG * J] for q in range(3))

        extra_deg = xb[:, :, :, :].rearrange("p a j d -> p (a j d)")[:, 0:NG * J * 2].rearrange("p (g j t) -> p g j t", j=J, t=2)
        xb_all = xb[:, :, :, :].rearrange("p a j d -> p (a j d)")
        deg_parts = xb_all[:, NG * J * 2:NG * J * (3 + PARTS)].rearrange("p (g j t) -> p g j t", j=J, t=PARTS + 1)
        fe_parts = xb_all[:, 0:NG * K * 2 * PARTS].rearrange("p (g k t h) -> p g k t h", k=K, t=2, h=PARTS)
        xe = sT[:, :, :, :].rearrange("p a j e -> p (a j e)").rearrange("p (u j d) -> p u j d", j=J, d=D)

        bank = [ctx.enter_context(nc.psum_tensor(f"bank{i}", [P, 512], f32)) for i in range(8)]

        def bj(i):
            return bank[i][:, 0:J * D].rearrange("p (j d) -> p j d", j=J)

        class PerGroup:

            def __init__(self, name, passes, per=1):
                self.sem, self.passes, self.per = sem(name), passes, per

            def at(self, p, g, k=None):
                return ((g + self.passes.index(p) * NG) * self.per) + (self.per if k is None else k)

        weights_in = sem("weights_in")
        edges_in = sem("edges_in")
        consts = sem("consts")
        dve_own = sem("dve_own")
        cnt_done = sem("cnt_done")
        sums_done = sem("sums_done")
        rec_done = sem("rec_done")
        roots_done = sem("roots_done")
        e0_sum = sem("e0_sum")
        wsT_done = sem("wsT_done")
        wsT_copied = sem("wsT_copied")
        e0_ready = sem("e0_ready")
        attr_in = [sem(f"attr_in{i}") for i in range(2)]
        attr_mul = sem("attr_mul")
        attr_sq = sem("attr_sq")
        sum_used = sem("sum_used")
        pads_out = sem("pads_out")
        rec_out = sem("rec_out")
        idx_ready = sem("idx_ready")
        gat_in = [sem(f"gat_in{i}") for i in range(4)]
        gat_started = sem("gat_started")
        roh_ready = sem("roh_ready")
        msg_T = sem("msg_T")
        msg_Tc = sem("msg_Tc")
        msg_Z = sem("msg_Z")
        msg_act = sem("msg_act")
        msg_sel = sem("msg_sel")
        msg_sum = sem("msg_sum")
        msg_out = [sem(f"msg_out{i}") for i in range(2)]
        xa_in = [sem(f"xa_in{i}") for i in range(RING)]
        side_in = [sem(f"side_in{i}") for i in range(RING)]
        rec_in = [sem(f"rec_in{i}") for i in range(RING)]
        G_in = [sem(f"G_in{i}") for i in range(RING)]
        stored = [sem(f"stored{i}") for i in range(4)]
        aggr_started = sem("aggr_started")
        slot_free = sem("slot_free")
        table_ready = sem("table_ready")
        bias_cut_done = sem("bias_cut_done")
        bias_out = sem("bias_out")
        bias_in = sem("bias_in")
        flag_ready = sem("flag_ready")
        flag_sum = sem("flag_sum")
        cleared = sem("cleared")
        clear_done = sem("clear_done")
        chunk_go = sem("chunk_go")
        one_own = sem("one_own")
        one_diag = sem("one_diag")
        one_bc = sem("one_bc")
        one_row = sem("one_row")
        one_idx = sem("one_idx")
        one_msg = sem("one_msg")
        one_src = sem("one_src")
        one_dst = sem("one_dst")
        one_val = sem("one_val")
        one_sum = sem("one_sum")
        one_tot = sem("one_tot")
        one_added = sem("one_added")
        one_wc = sem("one_wc")
        walk_set = sem("walk_set")
        lower_made = sem("lower_made")
        one_T = sem("one_T")
        one_Tc = sem("one_Tc")
        one_hid = sem("one_hid")
        one_hh = sem("one_hh")
        one_log = sem("one_log")
        one_th = sem("one_th")
        extra_ready = sem("extra_ready")
        xe_in = [sem(f"xe_in{i}") for i in range(4)]
        nums_out = sem("nums_out")
        deg_in = sem("deg_in")
        deg_all = sem("deg_all")
        ALLP = (0, 1, 2, 4, 5, 6)
        drel_done = PerGroup("drel_done", (0,))
        S_done = PerGroup("S_done", ALLP)
        agg_done = PerGroup("agg_done", (5, 6))
        T_done = PerGroup("T_done", (0, 1, 2, 4))
        Tc_done = PerGroup("Tc_done", (0, 1, 2, 4))
        H_done = PerGroup("H_done", (0, 1, 4))
        sum_done = PerGroup("sum_done", (1, 4))
        base_done = PerGroup("base_done", (0,))
        gam_done = PerGroup("gam_done", (0,))
        mid_done = PerGroup("mid_done", (0,))
        diag_done = PerGroup("diag_done", (4,))
        NORM = (0, 1, 4, 6)
        bn_done = PerGroup("bn_done", NORM)
        var_done = PerGroup("var_done", NORM)
        sd_done = PerGroup("sd_done", NORM)
        rs_done = PerGroup("rs_done", NORM)
        nb_done = PerGroup("nb_done", NORM)
        bn0_done = PerGroup("bn0_done", (0,))
        var0_done = PerGroup("var0_done", (0,))
        sd0_done = PerGroup("sd0_done", (0,))
        rs0_done = PerGroup("rs0_done", (0,))
        nb0_done = PerGroup("nb0_done", (0,))
        n0_done = PerGroup("n0_done", (0,))
        o_done = PerGroup("o_done", (0, 1, 3, 4, 5, 6))
        bc_done = PerGroup("bc_done", (2, 3))
        sT_done = PerGroup("sT_done", (2, 3))
        xd_done = PerGroup("xd_done", (2,))
        xdc_done = PerGroup("xdc_done", (2,))
        hp_done = PerGroup("hp_done", (2,))
        hh_done = PerGroup("hh_done", (2,))
        ep_done = PerGroup("ep_done", (2,))
        th_done = PerGroup("th_done", (2,))
        ew_done = PerGroup("ew_done", (2,))
        cut_done = PerGroup("cut_done", (2,), 3)
        dg_done = PerGroup("dg_done", (2,))
        fm_done = PerGroup("fm_done", (3,))
        fe_done = PerGroup("fe_done", (3,))
        deg_done = PerGroup("deg_done", (2,))
        dinv_ready = sem("dinv_ready")
        NEWTON = 3

        def uses(u, ring):
            return (NG - u + ring - 1) // ring

        def run_steps(eng, stages):
            lags = [lag for lag, _ in stages]
            top = NG - 1 + max(lags)
            blocks = (NG - 1) // RING
            peel = 1 if max(lags) + 4 <= RING else 2
            for s in range(RING * peel):
                for lag, stage in stages:
                    if s >= lag:
                        stage(s - lag, (s - lag) % RING, (s - lag) // RING)
            with eng.Fori(peel, blocks) as i:
                for s in range(RING):
                    for lag, stage in stages:
                        stage(i * RING + (s - lag), (s - lag) % RING, i + (s - lag) // RING)
            for s in range(blocks * RING, top + 1):
                for lag, stage in stages:
                    if 0 <= s - lag < NG:
                        stage(s - lag, (s - lag) % RING, (s - lag) // RING)

        def run_batches(eng, batch):
            batch(0, 0, 0)
            batch(1, 1, 0)
            with eng.Fori(1, NB // 2) as i:
                for par in range(2):
                    batch(i * 2 + par, par, i)
            batch(NB - 1, 0, NB // 2)

        def cut(g, size):
            return slice(g * size, (g + 1) * size) if isinstance(g, int) else bass.ds(g * size, size)

        def early(g, k):
            return isinstance(g, int) and g < k

        PASS = [dict(gather=None, a=x, b=None, out=x1),
                dict(gather=x1, a=x1, b=None, out=x2),
                dict(gather=x2, a=x2, b=None, out=None),
                dict(gather=None, a=x2, b=None, out=x2s),
                dict(gather=x2s, a=x2, b=None, out=x3),
                dict(gather=x3, a=x3, b=None, out=h1),
                dict(gather=h1, a=h1, b=x3, out=out)]
        A_PASSES = [p for p, ps in enumerate(PASS) if ps["a"] is not None]
        G_PASSES = [p for p, ps in enumerate(PASS) if ps["gather"] is not None]
        O_PASSES = [p for p, ps in enumerate(PASS) if ps["out"] is not None]
        STORE_LAG = [12, 12, None, None, 12, None, None]
        REC_PASSES = [0] + G_PASSES
        DROW_PASSES = [2, 3]
        FREE = {0: (base_done, H_done), 1: (sum_done,), 2: (xd_done,), 3: (bc_done, o_done), 4: (sum_done,), 5: (agg_done,), 6: (agg_done,)}

        def rec_count(p, u, n):
            return (n + REC_PASSES.index(p) * uses(u, RING)) * 16 + 16

        def G_count(p, u, n):
            return (n + G_PASSES.index(p) * uses(u, RING)) * 16 * K + 16 * K

        def xa_count(p, u, n):
            tail = 16 if u == (NG - 1) % RING and (p > 0 or (isinstance(n, int) and n == NG // RING)) else 0
            return (n + A_PASSES.index(p) * uses(u, RING)) * 16 + 16 + tail

        def side_count(p, u, n):
            return (n + (0, 2, 3, 6).index(p) * uses(u, RING)) * 16 + 16

        def stored_before(p, u, n):
            return (n * 2 + u // 4 + O_PASSES.index(p) * uses(u % 4, 4)) * 16

        full, rest = LAST // J, LAST % J

        def store_of(eng, p):
            def stage(g, u, n):
                eng.wait_ge(o_done.sem, o_done.at(p, g))
                rows = flat(o, u % 4)
                if p == len(PASS) - 1 and isinstance(g, int) and g == NG - 1:
                    r0 = g * GN
                    eng.dma_start(out[r0:r0 + full * J, :].rearrange("(p j) d -> p (j d)", j=J), rows[0:full, :]).then_inc(stored[u % 4], 16)
                    eng.dma_start(out[r0 + full * J:N, :].rearrange("(p j) d -> p (j d)", j=rest),
                                  rows[full:full + 1, 0:rest * D]).then_inc(stored[u % 4], 16)
                else:
                    eng.dma_start(PASS[p]["out"][cut(g, GN), :].rearrange("(p j) d -> p (j d)", j=J), rows).then_inc(stored[u % 4], 16)
            return stage

        def flat(ring, u):
            return ring[:, u, :, :].rearrange("p j d -> p (j d)")

        def flat_S(u, k):
            return S[:, u, k, :, :].rearrange("p j n -> p (j n)")

        def col(table, g):
            return table[:, g, :] if isinstance(g, int) else table[:, bass.ds(g, 1), :].rearrange("p a w -> p (a w)")

        def S16(u, k):
            return S[:, u, k, :, :].rearrange("p j n -> p (j n)").bitcast(bf16)[:, 0:GN].rearrange("p (j n) -> p j n", j=J)

        def sT16(u, j):
            return sT[:, u % 2, j, :].bitcast(bf16)[:, 0:GE]

        def bias_row(q):
            return bias16[:, q, :, :].rearrange("t j d -> t (j d)")

        def r_slot(u):
            return r[:, u % 4, :, :]

        def cell(table, g, j, t=None):
            if t is None:
                return table[:, g, j:j + 1] if isinstance(g, int) else table[:, bass.ds(g, 1), j]
            return table[:, g, j, t:t + 1] if isinstance(g, int) else table[:, bass.ds(g, 1), j, t]

        PRE = (0, 1, 2, 4, 5, 6)
        XE_PASSES = (0, 1, 4, 5, 6)
        TABLE = [msg0, x1, x2, None, x2s, x3, h1]

        def xe_count(p, u, n):
            return (n * 2 + u // 4 + XE_PASSES.index(p) * uses(u % 4, 4)) * 16 + 16

        def flagged(eng):
            return eng.value_load(flag_i[0:1, 0:1], min_val=0, max_val=1)

        def chunk(p, c):
            return c + PRE.index(p) * EC

        def among(passes, p, c):
            return c + passes.index(p) * EC

        def start_of(p, c):
            return chunk(p, c) + PRE.index(p) + 1

        block = ctx.enter_context(nc.Block())

        @block.sync
        def _(sp):
            sp.dma_start(src_n[:, :], src.rearrange("(p c) -> p c", p=EP)).then_inc(edges_in, 16)
            sp.dma_start(dst_n[:, :], dst.rearrange("(p c) -> p c", p=EP)).then_inc(edges_in, 16)
            sp.dma_start(next_n[0:EP - 1, :], dst[EC:E].rearrange("(p c) -> p c", c=EC)[:, 0:1], allow_slow_non_contiguous=True).then_inc(edges_in, 16)
            sp.dma_start(next_n[EP - 1:EP, :], dst[E - 1:E].rearrange("(p c) -> p c", c=1)).then_inc(edges_in, 16)
            sp.dma_start(typ_n[:, :], edge_type.rearrange("(p c) -> p c", p=EP)).then_inc(edges_in, 16)

            def row(v):
                return v.rearrange("(a n) -> a n", a=1)

            loads = [(w_rel[:, :].rearrange("d (r o) -> d r o", r=R), rel_w.rearrange("r d o -> d r o")),
                     (b_rel[:, :], rel_b), (w_raw[:, :], w_self),
                     (gam[:, :], row(ln_g).to_broadcast((P, D))), (bet[:, :], row(ln_b).to_broadcast((P, D))),
                     (w1_sb[:, :], w1), (mw1[:, 0, :], mlp_w1[0:D, :]), (mw1[:, 1, :], mlp_w1[D:2 * D, :]),
                     (mb1[:, :], mlp_b1.rearrange("(n a) -> n a", a=1)), (mw2[:, :], mlp_w2),
                     (mb2[:, :], row(mlp_b2).to_broadcast((P, 1))), (cw[:, :], conv_w),
                     (qb[:, :], row(q_emb).to_broadcast((P, D)))]
            loads += [(bias_f[0:1, q, :], row(v)) for q, v in enumerate((b_self, b1, conv_b))]
            assert len(loads) == NW
            for to, fro in loads:
                sp.dma_start(to, fro).then_inc(weights_in, 16)

            sp.wait_ge(consts, 1)
            sp.dma_start(msg0[E:E + GE, :].rearrange("(p k) d -> p (k d)", k=K), zero_pad[:, :]).then_inc(pads_out, 16)
            sp.dma_start(rec[E:E + GE, :].rearrange("(p k) d -> p (k d)", k=K),
                         rec_pad[:, :, :].rearrange("p k d -> p (k d)")).then_inc(pads_out, 16)
            sp.dma_start(dst_parts[:, E:E + GE].rearrange("(a t) e -> a t e", a=1), dst_pad[:, :, :]).then_inc(pads_out, 16)
            sp.wait_ge(bias_cut_done, 1)
            sp.dma_start(bias_parts.rearrange("(a t) d -> a t d", a=1), bias_cut[:, :, :, :].rearrange("a t b d -> a t (b d)")).then_inc(bias_out, 16)
            sp.wait_ge(bias_out, 16)
            for j in range(J):
                sp.dma_start(bias16[:, :, j, :], bias_parts.rearrange("t (b d) -> t b d", b=3)).then_inc(bias_in, 16)

            attr_v = edge_attr.rearrange("(p c) d -> p (c d)", p=EP)

            def attr_batch(b, par, n):
                if not early(b, 2):
                    sp.wait_ge(attr_mul, b - 1)
                    sp.wait_ge(attr_sq, b - 1)
                for lo, hi in ((0, 112), (112, EP)):
                    sp.dma_start(attr[lo:hi, par, :], attr_v[lo:hi, cut(b, EB * D)]).then_inc(attr_in[par], 16)

            run_batches(sp, attr_batch)
            sp.wait_ge(rec_done, 1)
            sp.dma_start(rec[0:E, :].rearrange("(p c) d -> p (c d)", p=EP),
                         rec_n[:, :, :].rearrange("p c d -> p (c d)")).then_inc(rec_out, 16)
            for t, part in enumerate((dst_hi, dst_lo)):
                sp.dma_start(dst_parts[t, 0:E].rearrange("(p c) -> p c", p=EP), part[:, :]).then_inc(rec_out, 16)

            def msg_batch(b, par, n):
                sp.wait_ge(msg_sum, b * EB + EB)
                sp.dma_start(msg0[0:E, :].rearrange("(p c) d -> p (c d)", p=EP)[:, cut(b, EB * D)],
                             msum[:, par, :, :].rearrange("p c d -> p (c d)")).then_inc(msg_out[par], 16)

            run_batches(sp, msg_batch)
            sp.wait_ge(msg_out[0], 16 * (NB - NB // 2))
            sp.wait_ge(msg_out[1], 16 * (NB // 2))
            sp.wait_ge(rec_out, 48)
            sp.wait_ge(pads_out, 48)
            sp.wait_ge(e0_ready, 1)

            sp.wait_ge(flag_ready, 1)
            flag = flagged(sp)

            def walk(p):
                with sp.Fori(0, (NPAD + P) // P // K) as i:
                    sp.dma_start(extra.rearrange("(p r) d -> p (r d)", p=P)[:, cut(i, K * D)], zero_pad[:, :]).then_inc(cleared, 16)
                sp.wait_ge(cleared, (PRE.index(p) + 1) * 16 * ((NPAD + P) // P // K))
                if p == 4:
                    for j in range(J):
                        sp.dma_start(node_num.rearrange("(g p j) t -> p j g t", p=P, j=J)[:, j], node_tab[:, :, j, :],
                                     allow_slow_non_contiguous=True).then_inc(nums_out, 16)
                    sp.wait_ge(nums_out, 16 * J)
                sp.sem_inc(clear_done, 1)
                if p == 0:
                    with sp.Fori(0, EC) as c:
                        sp.wait_ge(chunk_go, start_of(0, c))
                        sp.sem_inc(slot_free, 1)
                        sp.dma_start(rows_s, msg0[0:E, :].rearrange("(p c) d -> p (c d)", p=EP)[:, cut(c, D)]).then_inc(one_msg, 16)
                sp.wait_ge(extra_ready, PRE.index(p) + 1)
                if p == 2:
                    for j in range(J):
                        sp.dma_start(extra_deg[:, :, j, :], extra[0:NPAD, 0:2].rearrange("(g p j) t -> p j g t", p=P, j=J)[:, j],
                                     allow_slow_non_contiguous=True).then_inc(deg_in, 16)

            for p, ps in enumerate(PASS):
                if p in PRE:
                    with sp.If(flag > 0):
                        walk(p)

                def load_extra(g, u, n, p=p):
                    used = {0: H_done, 1: T_done, 4: T_done, 5: agg_done, 6: agg_done}[p]
                    if not early(g, 4):
                        sp.wait_ge(used.sem, used.at(p, g - 4))
                        sp.sem_inc(slot_free, 1)
                    sp.dma_start(xe[:, u % 4, :, :].rearrange("p j d -> p (j d)"),
                                 extra[cut(g, GN), :].rearrange("(p j) d -> p (j d)", j=J)).then_inc(xe_in[u % 4], 16)

                def load(g, u, n, p=p, ps=ps):
                    last = isinstance(g, int) and g == NG - 1
                    if not early(g, RING):
                        for used in FREE[p]:
                            sp.wait_ge(used.sem, used.at(p, g - RING))
                            sp.sem_inc(slot_free, 1)
                    if p in REC_PASSES or p in DROW_PASSES:
                        e0 = sp.value_load(e0_row[0:1, cut(g, 1)], min_val=0, max_val=E)
                    if p in REC_PASSES:
                        sp.dma_start(wrec[:, u, :, :].rearrange("p k f -> p (k f)"),
                                     rec[bass.ds(e0, GE), :].rearrange("(p k) f -> p (k f)", k=K)).then_inc(rec_in[u], 16)
                    if p == 0:
                        sp.dma_start(flat(G, u), msg0[bass.ds(e0, GE), :].rearrange("(p k) d -> p (k d)", k=K)).then_inc(side_in[u], 16)
                    if p in DROW_PASSES:
                        sp.dma_start(drow[:, u, :], dst_parts[:, bass.ds(e0, GE)]).then_inc(side_in[u], 16)
                    if p == 0 and last:
                        r0 = g * GN
                        sp.dma_start(flat(xa, u)[0:full, :], x[r0:r0 + full * J, :].rearrange("(p j) d -> p (j d)", j=J)).then_inc(xa_in[u], 16)
                        sp.dma_start(flat(xa, u)[full:full + 1, 0:rest * D],
                                     x[r0 + full * J:N, :].rearrange("(p j) d -> p (j d)", j=rest)).then_inc(xa_in[u], 16)
                    elif ps["a"] is not None:
                        sp.dma_start(flat(xa, u), ps["a"][cut(g, GN), :].rearrange("(p j) d -> p (j d)", j=J)).then_inc(xa_in[u], 16)
                    if ps["b"] is not None:
                        sp.dma_start(flat(xb, u), ps["b"][cut(g, GN), :].rearrange("(p j) d -> p (j d)", j=J)).then_inc(side_in[u], 16)

                stores = [(STORE_LAG[p], store_of(sp, p))] if STORE_LAG[p] is not None else []
                if p in XE_PASSES:
                    with sp.If(flag > 0):
                        run_steps(sp, stores + [(4, load_extra), (0, load)])
                    with sp.Else():
                        run_steps(sp, [(0, load)] + stores)
                else:
                    run_steps(sp, [(0, load)] + stores)
                if ps["out"] is None:
                    sp.wait_ge(deg_done.sem, deg_done.at(2, NG - 1))
                for q in range(4):
                    tail = 16 if p == len(PASS) - 1 and (NG - 1) % 4 == q else 0
                    if ps["out"] is not None:
                        sp.wait_ge(stored[q], 16 * (O_PASSES.index(p) + 1) * uses(q, 4) + tail)
                sp.sem_inc(table_ready, 1)

        @block.gpsimd
        def _(pool):
            nc.gpsimd.memset(zero_pad[:, :], 0.0)
            nc.gpsimd.memset(dst_pad[:, 0, :], -256.0)
            nc.gpsimd.memset(dst_pad[:, 1, :], 255.0)
            nc.gpsimd.memset(rec_pad[:, :, 0:1], 0)
            nc.gpsimd.memset(rec_pad[:, :, 1:2].bitcast(f32), -1.0)
            nc.gpsimd.memset(rec_pad[:, :, 2:4], 0).then_inc(consts, 1)
            nc.gpsimd.memset(rec_n[:, :, 3:4], 0)
            nc.gpsimd.iota(trash_row[:, :], pattern=[[0, 1]], base=NPAD, channel_multiplier=1, allow_small_or_imprecise_dtypes=True)
            nc.gpsimd.memset(ident[:, :], 0.0)
            nc.gpsimd.memset(ones_row[:, :], 1.0)
            nc.gpsimd.memset(ones_col[:, :], 1.0)
            nc.gpsimd.memset(eps_col[:, :], EPS_LN)
            nc.gpsimd.memset(ew16[:, :, :, PARTS:PARTS + 1], 1.0)
            nc.gpsimd.memset(ones16[:, :], 1.0)
            nc.gpsimd.iota(node_iota[:, :, :], pattern=[[1, J], [J, P]], base=0, channel_multiplier=0, allow_small_or_imprecise_dtypes=True)
            nc.gpsimd.iota(group_base[:, :], pattern=[[GN, NG]], base=0, channel_multiplier=0, allow_small_or_imprecise_dtypes=True)
            nc.gpsimd.iota(node_id[:, :, :], pattern=[[GN, NG], [1, J]], base=0, channel_multiplier=J, allow_small_or_imprecise_dtypes=True)
            nc.gpsimd.iota(rel_iota[:, :], pattern=[[1, R]], base=0, channel_multiplier=0, allow_small_or_imprecise_dtypes=True).then_inc(consts, 1)
            nc.gpsimd.memset(half_ident[:, :], 0.0).then_inc(consts, 1)
            pool.wait_ge(consts, 3)
            nc.gpsimd.affine_select(out=half_ident[:, :], in_=half_ident[:, :], compare_op=ALU.not_equal, fill=0.5, base=0,
                                    pattern=[[-1, P]], channel_multiplier=1)
            nc.gpsimd.affine_select(out=ident[:, :], in_=ident[:, :], compare_op=ALU.not_equal, fill=1.0, base=0,
                                    pattern=[[-1, P]], channel_multiplier=1).then_inc(consts, 1)

            pool.wait_ge(edges_in, 80)

            def gather_batch(b, par, n):
                if not early(b, 1):
                    for q in range(4):
                        pool.wait_ge(gat_in[q], b * (16 * EB // 4))
                nc.gpsimd.tensor_copy(idx_b[:, par, :], src_n[:, cut(b, EB)]).then_inc(idx_ready, 1)
                for c in range(EB):
                    if c == 0:
                        pool.wait_ge(idx_ready, b + 1)
                    if not (early(b, 1) and c < 4):
                        pool.wait_ge(msg_T, b * EB + (c - 3))
                    pool.sem_inc(gat_started, 1)
                    pool.indirect_dma_start(gat[:, c % 4, :], None, x, bass.IndirectOffsetOnAxis(
                        ap=idx_b[:, par, c:c + 1], axis=0)).then_inc(gat_in[c % 4], 16)

            run_batches(pool, gather_batch)

            pool.wait_ge(flag_ready, 1)
            flag = flagged(pool)

            def walk(p):
                pool.wait_ge(clear_done, PRE.index(p) + 1)
                if p == 0:
                    nc.gpsimd.memset(lower, 1.0).then_inc(lower_made, 1)
                    pool.wait_ge(lower_made, 1)
                    nc.gpsimd.affine_select(out=lower, in_=lower, compare_op=ALU.is_gt, fill=0.0, base=0,
                                            pattern=[[-1, EP]], channel_multiplier=1).then_inc(lower_made, 1)
                    pool.wait_ge(lower_made, 2)
                pool.sem_inc(chunk_go, 1)
                with pool.Fori(0, EC) as c:
                    nc.gpsimd.tensor_copy(src_i[:, :], src_n[:, cut(c, 1)])
                    nc.gpsimd.tensor_copy(dst_i[:, :], dst_n[:, cut(c, 1)]).then_inc(one_idx, 1)
                    pool.wait_ge(one_idx, chunk(p, c) + 1)
                    pool.sem_inc(gat_started, 1)
                    if p != 0:
                        pool.indirect_dma_start(rows_s, None, TABLE[p], bass.IndirectOffsetOnAxis(ap=src_i[:, 0:1], axis=0)).then_inc(one_src, 16)
                    if p == 2:
                        pool.indirect_dma_start(rows_d, None, TABLE[p], bass.IndirectOffsetOnAxis(ap=dst_i[:, 0:1], axis=0)).then_inc(one_dst, 16)
                    if p == 4:
                        pool.indirect_dma_start(nums[:, :], None, node_num, bass.IndirectOffsetOnAxis(ap=dst_i[:, 0:1], axis=0)).then_inc(one_dst, 16)
                    pool.wait_ge(one_row, chunk(p, c) + 1)
                    pool.sem_inc(gat_started, 1)
                    pool.wait_ge(one_tot, chunk(p, c) + 1)
                    pool.sem_inc(gat_started, 1)
                    pool.indirect_dma_start(extra, bass.IndirectOffsetOnAxis(ap=row_i[:, 0:1], axis=0), tot, None,
                                            compute_op=ALU.add).then_inc(one_added, 16)
                    pool.wait_ge(one_added, (chunk(p, c) + 1) * 16)
                    pool.sem_inc(chunk_go, 1)
                pool.sem_inc(extra_ready, 1)

            with pool.If(flag > 0):
                walk(0)

            def base(g, u, n):
                pool.wait_ge(xa_in[u], xa_count(0, u, n))
                nc.gpsimd.tensor_tensor(out=xb[:, u, :, :], in0=xa[:, u, :, :], in1=bet[:, :].unsqueeze(1).to_broadcast((P, J, D)),
                                        op=ALU.add).then_inc(base_done.sem, 1)

            def times_gamma(g, u, n):
                pool.wait_ge(n0_done.sem, n0_done.at(0, g))
                nc.gpsimd.tensor_tensor(out=hx[:, u % 4, :, :], in0=hx[:, u % 4, :, :], in1=gam[:, :].unsqueeze(1).to_broadcast((P, J, D)),
                                        op=ALU.mult).then_inc(gam_done.sem, 1)

            def mid(g, u, n):
                pool.wait_ge(base_done.sem, base_done.at(0, g))
                pool.wait_ge(gam_done.sem, gam_done.at(0, g))
                if not early(g, 4):
                    pool.wait_ge(o_done.sem, o_done.at(0, g - 4))
                nc.gpsimd.tensor_tensor(out=flat(r, u % 4), in0=flat(hx, u % 4), in1=flat(xb, u), op=ALU.add).then_inc(mid_done.sem, 1)

            run_steps(pool, [(6, times_gamma), (2, base), (6, mid)])

            for p, ps in enumerate(PASS):
                if ps["gather"] is None:
                    continue
                with pool.If(flag > 0):
                    walk(p)
                pool.wait_ge(table_ready, p)

                def gather(g, u, n, p=p, ps=ps):
                    pool.wait_ge(rec_in[u], rec_count(p, u, n))
                    pool.sem_inc(gat_started, 1)
                    for k in range(K):
                        pool.indirect_dma_start(G[:, u, k, :], None, ps["gather"], bass.IndirectOffsetOnAxis(
                            ap=wrec[:, u, k, 0:1], axis=0)).then_inc(G_in[u], 16)

                run_steps(pool, [(0, gather)])

        @block.scalar
        def _(act):
            def square(b, par, n):
                act.wait_ge(attr_in[par], n * 32 + 32)
                if not early(b, 2):
                    act.wait_ge(sum_used, b - 1)
                nc.scalar.activation(prod2[:, par, :], attr[:, par, :], ACT.Square).then_inc(attr_sq, 1)

            run_batches(act, square)
            act.wait_ge(sums_done, 1)
            nc.scalar.activation(nrm[:, :], ssq[:, :], ACT.Sqrt)
            nc.scalar.activation(qn[:, 1:2], qn[:, 0:1], ACT.Sqrt).then_inc(roots_done, 1)
            act.wait_ge(wsT_done, 1)
            nc.scalar.activation(w_selfT[:, :], bank[1][:, 0:D], ACT.Copy).then_inc(wsT_copied, 1)

            def msg_copy(n, c2):
                act.wait_ge(msg_T, n + 1)
                nc.scalar.activation(gatT[:, c2, :], bank[7 * c2][:, 0:EP], ACT.Copy)
                nc.scalar.activation(rohT[:, c2, :], bank[7 * c2][0:R, P:P + EP], ACT.Copy).then_inc(msg_Tc, 1)

            def msg_pick(n, c2, par, c):
                act.wait_ge(msg_Z, n + 1)
                if not early(n, 2):
                    act.wait_ge(msg_sum, n - 1)
                for q, (lo, hi) in enumerate(REL_CUT[1:]):
                    for r_ in range(lo, hi):
                        nc.scalar.activation(sel[:, c2, r_, :], bank[2 + q + 3 * c2][0:EP, (r_ - lo) * D:(r_ - lo + 1) * D],
                                             ACT.Copy, scale=roh[:, par, c, r_:r_ + 1])
                lo = REL_CUT[2][0]
                nc.scalar.activation(sel[:, c2, R, :], bank[3 + 3 * c2][0:EP, (R - lo) * D:(R + 1 - lo) * D], ACT.Copy).then_inc(msg_act, 1)

            def msg_steps(b, par, nb_):
                for c in range(EB):
                    msg_copy(b * EB + c, c % 2)
                    if not (early(b, 1) and c == 0):
                        msg_pick(b * EB + (c - 1), (c - 1) % 2, par if c else 1 - par, (c - 1) % EB)

            run_batches(act, msg_steps)
            msg_pick(EC - 1, (EC - 1) % 2, (NB - 1) % 2, EB - 1)

            act.wait_ge(flag_ready, 1)
            flag = flagged(act)

            def walk():
                gT1, dT1, hh1, th1 = gT[:, 0, 0, 0:EP], gT[:, 1, 0, 0:EP], hh[:, 0, 0, 0:EP], th[0:EP, 0, 0:1]
                with act.Fori(0, EC) as c:
                    act.wait_ge(one_T, c + 1)
                    nc.scalar.activation(gT1, bank[0][:, 0:EP], ACT.Copy)
                    nc.scalar.activation(dT1, bank[0][:, P:P + EP], ACT.Copy).then_inc(one_Tc, 1)
                    act.wait_ge(one_hid, c + 1)
                    nc.scalar.activation(hh1, bank[4][0:H, 0:EP], ACT.Gelu, bias=mb1[:, 0:1]).then_inc(one_hh, 1)
                    act.wait_ge(one_log, c + 1)
                    nc.scalar.activation(th1, bank[5][0:EP, 0:1], ACT.Tanh, scale=0.5, bias=mb2h[0:EP, 0:1]).then_inc(one_th, 1)

            def normed(p, source):
                def stage(g, u, n):
                    act.wait_ge(nb_done.sem, nb_done.at(p, g))
                    if not (p == 0 and early(g, 4)):
                        act.wait_ge(stored[u % 4], stored_before(p, u, n))
                    for j in range(J):
                        ins = nc.scalar.activation(o[:, u % 4, j, :], source(u)[:, j, :], ACT.Identity,
                                                   scale=rsb[:, u % 4, j:j + 1], bias=nbb[:, u % 4, j:j + 1])
                    ins.then_inc(o_done.sem, 1)
                return stage

            def sd(p, var, to, m, done):
                def stage(g, u, n):
                    act.wait_ge(var.sem, var.at(p, g))
                    nc.scalar.activation(to[:, u % 4, :], m[:, u % 4, :, 1], ACT.Sqrt, bias=eps_col[:, 0:1]).then_inc(done.sem, 1)
                return stage

            def sd_out(p):
                return sd(p, var_done, sdb, mvb, sd_done)

            def copy_T(p):
                def stage(g, u, n):
                    act.wait_ge(T_done.sem, T_done.at(p, g))
                    nc.scalar.activation(flat(yT, u % 4), bank[u % 2][:, 0:J * D], ACT.Copy).then_inc(Tc_done.sem, 1)
                return stage

            def normed0(g, u, n):
                act.wait_ge(nb0_done.sem, nb0_done.at(0, g))
                if not early(g, 4):
                    act.wait_ge(mid_done.sem, mid_done.at(0, g - 4))
                for j in range(J):
                    ins = nc.scalar.activation(hx[:, u % 4, j, :], bj(2 + u % 4)[:, j, :], ACT.Identity,
                                               scale=rsa[:, u % 4, j:j + 1], bias=nba[:, u % 4, j:j + 1])
                ins.then_inc(n0_done.sem, 1)

            run_steps(act, [(6, normed0), (1, copy_T(0)), (4, sd(0, var0_done, sda, mva, sd0_done)), (8, sd_out(0)), (9, normed(0, r_slot))])
            run_steps(act, [(6, normed(1, r_slot)), (1, copy_T(1)), (4, sd_out(1))])

            with act.If(flag > 0):
                walk()

            def gT_copy(g, u, n):
                act.wait_ge(T_done.sem, T_done.at(2, g))
                nc.scalar.activation(flat(gT, u % 4), bank[0][:, 0:GE], ACT.Copy).then_inc(Tc_done.sem, 1)

            def xdT_copy(g, u, n):
                act.wait_ge(xd_done.sem, xd_done.at(2, g))
                nc.scalar.activation(xdT[:, u % 2, :], bank[3][:, 0:GE], ACT.Copy).then_inc(xdc_done.sem, 1)

            def gelu(g, u, n):
                act.wait_ge(hp_done.sem, hp_done.at(2, g))
                nc.scalar.activation(flat(hh, u % 4), bank[4][0:H, 0:GE], ACT.Gelu, bias=mb1[:, 0:1]).then_inc(hh_done.sem, 1)

            def edge_tanh(g, u, n):
                act.wait_ge(ep_done.sem, ep_done.at(2, g))
                nc.scalar.activation(th[:, u % 4, :], bank[5][:, 0:K], ACT.Tanh, scale=0.5, bias=mb2h[:, 0:1]).then_inc(th_done.sem, 1)

            run_steps(act, [(5, edge_tanh), (4, gelu), (3, xdT_copy), (2, gT_copy)])

            act.wait_ge(dinv_ready, 1)

            def scaled_rows(g, u, n):
                act.wait_ge(xa_in[u], xa_count(3, u, n))
                act.wait_ge(stored[u % 4], stored_before(3, u, n))
                for j in range(J):
                    ins = nc.scalar.activation(o[:, u % 4, j, :], xa[:, u, j, :], ACT.Copy, scale=cell(node_tab, g, j, 0))
                ins.then_inc(o_done.sem, 1)

            run_steps(act, [(2, store_of(act, 3)), (1, scaled_rows)])

            def diagonal(g, u, n):
                if not early(g, 4):
                    act.wait_ge(T_done.sem, T_done.at(4, g - 4))
                for j in range(J):
                    ins = nc.scalar.activation(r[:, u % 4, j, :], ident[:, :], ACT.Copy, scale=cell(dinv2_tab, g, j))
                ins.then_inc(diag_done.sem, 1)

            run_steps(act, [(0, diagonal), (2, copy_T(4)), (5, sd_out(4)), (7, normed(4, lambda u: hx[:, u % 4, :, :]))])

            def h1_out(g, u, n):
                act.wait_ge(agg_done.sem, agg_done.at(5, g))
                act.wait_ge(stored[u % 4], stored_before(5, u, n))
                nc.scalar.activation(flat(o, u % 4), bank[u % 4][:, 0:J * D], ACT.Copy).then_inc(o_done.sem, 1)

            run_steps(act, [(3, store_of(act, 5)), (2, h1_out)])
            run_steps(act, [(6, store_of(act, 6)), (5, normed(6, lambda u: bj(u % 4))), (3, sd_out(6))])

        @block.vector
        def _(dve):
            chain = [0]

            def link(ins):
                chain[0] += 1
                ins.then_inc(dve_own, 1)
                dve.wait_ge(dve_own, chain[0])

            dve.wait_ge(edges_in, 80)
            nc.vector.tensor_copy(dstf[:, :], dst_n[:, :])
            link(nc.vector.tensor_copy(typf[:, :], typ_n[:, :]))
            dve.wait_ge(consts, 2)
            nc.vector.tensor_tensor(out=rel_1h[:, :, :], in0=typf[:, :].unsqueeze(2).to_broadcast((EP, EC, R)),
                                    in1=rel_iota[0:EP, :].unsqueeze(1).to_broadcast((EP, EC, R)), op=ALU.is_equal)
            for b0 in range(0, NG, CB):
                w = min(CB, NG - b0)
                link(nc.vector.tensor_tensor(out=cmp_t[:, 0:w, :], in0=dstf[:, :].unsqueeze(1).to_broadcast((EP, w, EC)),
                                             in1=group_base[0:EP, b0:b0 + w].unsqueeze(2).to_broadcast((EP, w, EC)), op=ALU.is_lt))
                link(nc.vector.tensor_reduce(out=cnt[:, b0:b0 + w], in_=cmp_t[:, 0:w, :], axis=AX.X, op=ALU.add))
            nc.vector.tensor_copy(next_f[:, :], next_n[:, :])
            link(nc.vector.tensor_tensor(out=cmp_t[:, 0, 0:EC - 1], in0=dstf[:, 1:EC], in1=dstf[:, 0:EC - 1], op=ALU.is_lt))
            link(nc.vector.tensor_tensor(out=cmp_t[:, 0, EC - 1:EC], in0=next_f[:, :], in1=dstf[:, EC - 1:EC], op=ALU.is_lt))
            link(nc.vector.tensor_reduce(out=cnt[:, NG:NG + 1], in_=cmp_t[:, 0, :], axis=AX.X, op=ALU.add))
            dve.sem_inc(cnt_done, 1)
            dve.wait_ge(e0_sum, 1)
            nc.vector.tensor_copy(e0_row[:, :], bank[0][0:1, 0:NG]).then_inc(e0_ready, 1)
            link(nc.vector.tensor_copy(size_row[:, :], bank[0][0:1, 0:NG + 1]))
            nc.vector.tensor_scalar(flag_f[:, 1:2], size_row[:, NG:NG + 1], 0.0, None, ALU.is_gt)
            link(nc.vector.tensor_scalar(size_row[:, NG:NG + 1], size_row[:, NG:NG + 1], 0.0, float(E), ALU.mult, ALU.add))
            link(nc.vector.tensor_tensor(out=cnt[0:1, 0:NG], in0=size_row[:, 1:NG + 1], in1=size_row[:, 0:NG], op=ALU.subtract))
            link(nc.vector.tensor_reduce(out=flag_f[:, 0:1], in_=cnt[0:1, 0:NG], axis=AX.X, op=ALU.max))
            link(nc.vector.tensor_scalar(flag_f[:, 0:1], flag_f[:, 0:1], float(GE), None, ALU.is_gt))
            link(nc.vector.tensor_tensor(out=flag_f[:, 0:1], in0=flag_f[:, 0:1], in1=flag_f[:, 1:2], op=ALU.max))
            nc.vector.tensor_copy(flag_i[:, :], flag_f[:, 0:1]).then_inc(flag_ready, 1)
            dve.wait_ge(flag_sum, 1)
            link(nc.vector.tensor_copy(flag_col[:, :], bank[2][0:EP, 0:1]))

            dve.wait_ge(weights_in, 16 * NW)
            link(nc.vector.tensor_copy(bias_cut[:, 0, :, :], bias_f[:, :, :]))
            link(nc.vector.tensor_tensor(out=bias_rest[:, :, :], in0=bias_f[:, :, :], in1=bias_cut[:, 0, :, :], op=ALU.subtract))
            link(nc.vector.tensor_copy(bias_cut[:, 1, :, :], bias_rest[:, :, :]))
            nc.vector.tensor_tensor(out=bias_cut[:, 2, :, :], in0=bias_rest[:, :, :], in1=bias_cut[:, 1, :, :], op=ALU.subtract).then_inc(bias_cut_done, 1)

            dve.wait_ge(weights_in, 16 * NW)
            nc.vector.tensor_scalar(mb2h[:, :], mb2[:, :], 0.5, None, ALU.mult)
            link(nc.vector.tensor_tensor(out=qsq[:, :], in0=qb[:, :], in1=qb[:, :], op=ALU.mult))
            link(nc.vector.tensor_reduce(out=qn[:, 0:1], in_=qsq[:, :], axis=AX.X, op=ALU.add))

            def attr_batch(b, par, n):
                dve.wait_ge(attr_in[par], n * 32 + 32)
                nc.vector.tensor_tensor(out=prod[:, par, :].rearrange("p (c d) -> p c d", d=D),
                                        in0=attr[:, par, :].rearrange("p (c d) -> p c d", d=D),
                                        in1=qb[0:EP, :].unsqueeze(1).to_broadcast((EP, EB, D)), op=ALU.mult).then_inc(attr_mul, 1)
                dve.wait_ge(attr_sq, b + 1)
                nc.vector.tensor_reduce(out=ssq[:, cut(b, EB)], in_=prod2[:, par, :].rearrange("p (c d) -> p c d", d=D),
                                        axis=AX.X, op=ALU.add).then_inc(sum_used, 1)
                dve.wait_ge(attr_mul, b + 1)
                nc.vector.tensor_reduce(out=dotq[:, cut(b, EB)], in_=prod[:, par, :].rearrange("p (c d) -> p c d", d=D), axis=AX.X, op=ALU.add)

            run_batches(dve, attr_batch)
            link(nc.vector.tensor_copy(qn[:, 3:4], qn[:, 0:1]))
            dve.sem_inc(sums_done, 1)
            dve.wait_ge(roots_done, 1)
            nc.vector.tensor_scalar(nrm[:, :], nrm[:, :], EPS_Q, None, ALU.max)
            link(nc.vector.tensor_scalar(qn[:, 1:2], qn[:, 1:2], EPS_Q, None, ALU.max))
            nc.vector.reciprocal(nrm[:, :], nrm[:, :])
            link(nc.vector.reciprocal(qn[:, 2:3], qn[:, 1:2]))
            link(nc.vector.tensor_scalar(dotq[:, :], dotq[:, :], qn[0:EP, 2:3], None, ALU.mult))
            dve.wait_ge(consts, 2)
            nc.vector.tensor_copy(rec_n[:, :, 0], src_n[:, :])
            link(nc.vector.tensor_scalar(typf[:, :], dstf[:, :], 1.0, flag_col[:, 0:1], ALU.add, ALU.mult))
            link(nc.vector.tensor_tensor(out=typf[:, :], in0=dstf[:, :], in1=typf[:, :], op=ALU.subtract))
            nc.vector.tensor_copy(rec_n[:, :, 1].bitcast(f32), typf[:, :])
            link(nc.vector.tensor_copy(typ_n[:, :], typf[:, :]))
            link(nc.vector.tensor_scalar(typ_n[:, :], typ_n[:, :], 255, None, ALU.bitwise_and))
            link(nc.vector.tensor_copy(ssq[:, :], typ_n[:, :]))
            nc.vector.tensor_copy(dst_lo[:, :], ssq[:, :])
            link(nc.vector.tensor_tensor(out=dst_hi[:, :], in0=typf[:, :], in1=ssq[:, :], op=ALU.subtract))
            nc.vector.tensor_tensor(out=rec_n[:, :, 2].bitcast(f32), in0=dotq[:, :], in1=nrm[:, :], op=ALU.mult).then_inc(rec_done, 1)

            def msg_total(n, par, c):
                dve.wait_ge(msg_sel, n + 1)
                dve.wait_ge(msg_act, n + 1)
                nc.vector.tensor_reduce(out=msum[:, par, c, :], in_=sel[:, c % 2, :, :].rearrange("p r d -> p d r"),
                                        axis=AX.X, op=ALU.add).then_inc(msg_sum, 1)

            def msg_steps(b, par, nb_):
                dve.wait_ge(roh_ready, b + 1)
                for c in range(EB):
                    n, c2 = b * EB + c, c % 2
                    dve.wait_ge(msg_Z, n + 1)
                    if not early(n, 2):
                        dve.wait_ge(msg_sum, n - 1)
                    lo, hi = REL_CUT[0]
                    nc.vector.tensor_tensor(
                        out=sel[:, c2, lo:hi, :], in0=bank[1 + 3 * c2][0:EP, 0:(hi - lo) * D].rearrange("p (r d) -> p r d", d=D),
                        in1=roh[:, par, c, lo:hi].unsqueeze(2).to_broadcast((EP, hi - lo, D)), op=ALU.mult).then_inc(msg_sel, 1)
                    if c == 1 and not early(b, 2):
                        dve.wait_ge(msg_out[par], nb_ * 16)
                    if not (early(b, 1) and c == 0):
                        msg_total(b * EB + (c - 1), par if c else 1 - par, (c - 1) % EB)
                    if c == 1 and not (isinstance(b, int) and b == NB - 1):
                        nc.vector.tensor_copy(roh[:, 1 - par, :, :], rel_1h[:, cut(b + 1, EB), :]).then_inc(roh_ready, 1)

            nc.vector.tensor_copy(roh[:, 0, :, :], rel_1h[:, 0:EB, :]).then_inc(roh_ready, 1)
            run_batches(dve, msg_steps)
            msg_total(EC - 1, (NB - 1) % 2, EB - 1)

            dve.wait_ge(flag_ready, 1)
            flag = flagged(dve)
            LINKS = 6

            def walk(p):
                dve.wait_ge(clear_done, PRE.index(p) + 1)
                if p == 0:
                    nc.vector.memset(ones_sq, 1.0).then_inc(walk_set, 1)
                    dve.wait_ge(walk_set, 1)
                if p == 2:
                    nc.vector.memset(val, 0.0).then_inc(walk_set, 1)
                    dve.wait_ge(walk_set, 2)
                    nc.vector.memset(val[:, 1:2], 1.0).then_inc(walk_set, 1)
                    dve.wait_ge(walk_set, 3)
                with dve.Fori(0, EC) as c:
                    step = [0]

                    def then(ins):
                        step[0] += 1
                        ins.then_inc(one_own, 1)
                        dve.wait_ge(one_own, chunk(p, c) * LINKS + step[0])

                    dve.wait_ge(chunk_go, start_of(p, c))
                    then(nc.vector.tensor_copy(own_dst[:, :], dstf[:, cut(c, 1)]))
                    nc.vector.tensor_scalar(diag_n, ident[0:EP, 0:EP], own_dst[:, 0:1], None, ALU.mult).then_inc(one_diag, 1)
                    dve.wait_ge(one_bc, chunk(p, c) + 1)
                    then(nc.vector.tensor_scalar(same, bank[1][0:EP, 0:EP], own_dst[:, 0:1], None, ALU.is_equal))
                    then(nc.vector.tensor_tensor(out=diag_n, in0=same, in1=lower, op=ALU.mult))
                    then(nc.vector.tensor_reduce(out=row_f[:, 0:1], in_=diag_n, axis=AX.X, op=ALU.add))
                    nc.vector.tensor_tensor(out=row_f[:, 2:3], in0=own_dst[:, :], in1=trash_row[:, :], op=ALU.subtract)
                    then(nc.vector.tensor_scalar(row_f[:, 1:2], row_f[:, 0:1], 0.0, None, ALU.is_equal))
                    then(nc.vector.scalar_tensor_tensor(out=row_f[:, 3:4], in0=row_f[:, 2:3], scalar=row_f[:, 1:2], in1=trash_row[:, :],
                                                        op0=ALU.mult, op1=ALU.add))
                    nc.vector.tensor_copy(row_i[:, :], row_f[:, 3:4]).then_inc(one_row, 1)
                    if p == 0:
                        dve.wait_ge(one_msg, c * 16 + 16)
                        ins = nc.vector.tensor_copy(val, rows_s)
                    elif p == 1:
                        dve.wait_ge(one_src, c * 16 + 16)
                        ins = nc.vector.tensor_copy(val, rows_s)
                    elif p == 2:
                        dve.wait_ge(one_th, c + 1)
                        nc.vector.tensor_scalar(ew_n[:, cut(c, 1)], th[0:EP, 0, 0:1], 0.5, 0.5, ALU.mult, ALU.add)
                        ins = nc.vector.tensor_scalar(val[:, 0:1], th[0:EP, 0, 0:1], 0.5, 0.5, ALU.mult, ALU.add)
                    else:
                        if p == 4:
                            dve.wait_ge(one_dst, (c + EC) * 16 + 16)
                            nc.vector.tensor_tensor(out=ws_n[:, cut(c, 1)], in0=rec_n[:, cut(c, 1), 2].bitcast(f32), in1=nums[:, 1:2], op=ALU.mult)
                            nc.vector.tensor_tensor(out=wc_n[:, cut(c, 1)], in0=ew_n[:, cut(c, 1)], in1=nums[:, 0:1], op=ALU.mult).then_inc(one_wc, 1)
                            dve.wait_ge(one_wc, c + 1)
                        dve.wait_ge(one_src, among((1, 2, 4, 5, 6), p, c) * 16 + 16)
                        ins = nc.vector.tensor_scalar(val, rows_s, (wc_n if p == 4 else ws_n)[:, cut(c, 1)], None, ALU.mult)
                    ins.then_inc(one_val, 1)
                    dve.wait_ge(one_sum, chunk(p, c) + 1)
                    nc.vector.tensor_copy(tot, bank[2][0:EP, 0:D]).then_inc(one_tot, 1)

            def walk_if_flagged(p):
                with dve.If(flag > 0):
                    walk(p)

            def drel_of(g, u, n):
                dve.wait_ge(rec_in[u], rec_count(0, u, n))
                nc.vector.tensor_copy(col(sim_tab, g), wrec[:, u, :, 2].bitcast(f32))
                nc.vector.tensor_scalar(col(drel_tab, g), wrec[:, u, :, 1].bitcast(f32), group_base[:, cut(g, 1)],
                                        None, ALU.subtract).then_inc(drel_done.sem, 1)

            def S_of(p, weight):
                def stage(g, u, n):
                    if p == 0:
                        dve.wait_ge(drel_done.sem, drel_done.at(0, g))
                    if p == 5 and not early(g, RING):
                        dve.wait_ge(agg_done.sem, agg_done.at(5, g - RING))
                    for k in range(K):
                        to = S16(u, k) if p == 2 else S[:, u, k, :, :]
                        w, op = (None, ALU.bypass) if weight is None else (cell(weight, g, k), ALU.mult)
                        ins = nc.vector.tensor_scalar(to, node_iota[:, :, :], cell(drel_tab, g, k), w, ALU.is_equal, op)
                    ins.then_inc(S_done.sem, 1)
                return stage

            class Norm:

                def __init__(self, p, ready, source, st, m, sdt, rst, nbt, bn, var, sd_, rs_, nb_):
                    self.p, self.ready, self.source, self.st, self.m, self.rst, self.nbt = p, ready, source, st, m, rst, nbt
                    self.sdt, self.bn_, self.var_, self.sd_, self.rs_, self.nb_ = sdt, bn, var, sd_, rs_, nb_

                def sums(self, g, u, n):
                    dve.wait_ge(self.ready.sem, self.ready.at(self.p, g))
                    for j in range(J):
                        ins = nc.vector.bn_stats(self.st[:, u % 4, j, :], self.source(u)[:, j, :])
                    ins.then_inc(self.bn_.sem, 1)

                def variance(self, g, u, n):
                    dve.wait_ge(self.bn_.sem, self.bn_.at(self.p, g))
                    dve.sem_inc(aggr_started, 1)
                    for j in range(J):
                        ins = nc.vector.bn_aggr(self.m[:, u % 4, j, :], self.st[:, u % 4, j, :])
                    ins.then_inc(self.var_.sem, 1)

                def inverse(self, g, u, n):
                    dve.wait_ge(self.sd_.sem, self.sd_.at(self.p, g))
                    nc.vector.reciprocal(self.rst[:, u % 4, :], self.sdt[:, u % 4, :]).then_inc(self.rs_.sem, 1)

                def offset(self, g, u, n):
                    dve.wait_ge(self.rs_.sem, self.rs_.at(self.p, g))
                    nc.vector.scalar_tensor_tensor(out=self.nbt[:, u % 4, :], in0=self.m[:, u % 4, :, 0], scalar=-1.0,
                                                   in1=self.rst[:, u % 4, :], op0=ALU.mult, op1=ALU.mult).then_inc(self.nb_.sem, 1)

            def norm_out(p, ready, source):
                return Norm(p, ready, source, st6b, mvb, sdb, rsb, nbb, bn_done, var_done, sd_done, rs_done, nb_done)

            walk_if_flagged(0)
            inner = Norm(0, H_done, lambda u: bj(2 + u % 4), st6a, mva, sda, rsa, nba, bn0_done, var0_done, sd0_done, rs0_done, nb0_done)
            outer = norm_out(0, mid_done, r_slot)
            run_steps(dve, [(5, inner.inverse), (9, outer.inverse), (4, inner.sums), (8, outer.sums), (1, S_of(0, None)), (5, inner.offset),
                            (9, outer.offset), (4, inner.variance), (8, outer.variance), (0, drel_of)])

            def relu_sum(g, u, n):
                dve.wait_ge(H_done.sem, H_done.at(1, g))
                if not early(g, 4):
                    dve.wait_ge(o_done.sem, o_done.at(1, g - 4))
                nc.vector.scalar_tensor_tensor(out=flat(r, u % 4), in0=bank[2 + u % 2][:, 0:J * D], scalar=0.0,
                                               in1=flat(xa, u), op0=ALU.max, op1=ALU.add).then_inc(sum_done.sem, 1)

            walk_if_flagged(1)
            outer = norm_out(1, sum_done, r_slot)
            run_steps(dve, [(5, outer.inverse), (4, outer.variance), (3, relu_sum), (0, S_of(1, None)), (5, outer.offset), (3, outer.sums)])

            def sT_of(p, used):
                def stage(g, u, n):
                    dve.wait_ge(bc_done.sem, bc_done.at(p, g))
                    if not early(g, 2):
                        dve.wait_ge(used.sem, used.at(p, g - 2))
                    for j in range(J):
                        ins = nc.vector.tensor_scalar(sT16(u, j) if p == 3 else sT[:, u % 2, j, :], bank[6 + u % 2][:, 0:GE], cell(node_id, g, j), None, ALU.is_equal)
                    ins.then_inc(sT_done.sem, 1)
                return stage

            def edge_weight(g, u, n):
                dve.wait_ge(th_done.sem, th_done.at(2, g))
                nc.vector.tensor_scalar(ew16[:, u % 4, :, 0], th[:, u % 4, :], 0.5, 0.5, ALU.mult, ALU.add)
                nc.vector.tensor_scalar(col(ew_tab, g), th[:, u % 4, :], 0.5, 0.5, ALU.mult, ALU.add).then_inc(cut_done.sem, 1)

            def edge_rest(g, u, n):
                dve.wait_ge(cut_done.sem, cut_done.at(2, g, 1))
                nc.vector.tensor_tensor(out=ew_rest[:, u % 4, :], in0=col(ew_tab, g), in1=ew16[:, u % 4, :, 0], op=ALU.subtract).then_inc(cut_done.sem, 1)

            def edge_mid(g, u, n):
                dve.wait_ge(cut_done.sem, cut_done.at(2, g, 2))
                nc.vector.tensor_copy(ew16[:, u % 4, :, 1], ew_rest[:, u % 4, :]).then_inc(cut_done.sem, 1)

            def edge_low(g, u, n):
                dve.wait_ge(cut_done.sem, cut_done.at(2, g, 3))
                nc.vector.tensor_tensor(out=ew16[:, u % 4, :, 2], in0=ew_rest[:, u % 4, :], in1=ew16[:, u % 4, :, 1],
                                        op=ALU.subtract).then_inc(ew_done.sem, 1)

            def degree_copy(g, u, n):
                dve.wait_ge(dg_done.sem, dg_done.at(2, g))
                to = deg_parts[:, g, :, :] if isinstance(g, int) else deg_parts[:, bass.ds(g, 1), :, :].rearrange("p a j t -> p (a j) t")
                nc.vector.tensor_copy(to, bank[1 + u % 2][:, 0:(PARTS + 1) * J].rearrange("p (j t) -> p j t", j=J)).then_inc(deg_done.sem, 1)

            walk_if_flagged(2)
            run_steps(dve, [(7, edge_weight), (9, degree_copy), (7, edge_rest), (2, sT_of(2, xd_done)), (7, edge_mid), (1, S_of(2, None)), (7, edge_low)])

            dve.wait_ge(deg_done.sem, deg_done.at(2, NG - 1))
            sums2 = deg_tab[:, :, :, :].rearrange("p g j t -> p (g j) t")
            parts2 = deg_parts.rearrange("p g j t -> p (g j) t")
            nc.vector.tensor_copy(sums2[:, :, 1], parts2[:, :, PARTS])
            link(nc.vector.tensor_tensor(out=nt_a[:, :], in0=parts2[:, :, 1], in1=parts2[:, :, 2], op=ALU.add))
            link(nc.vector.tensor_tensor(out=sums2[:, :, 0], in0=parts2[:, :, 0], in1=nt_a[:, :], op=ALU.add))
            with dve.If(flag > 0):
                dve.wait_ge(deg_in, 16 * J)
                nc.vector.tensor_tensor(out=deg_tab[:, :, :, :], in0=deg_tab[:, :, :, :], in1=extra_deg, op=ALU.add).then_inc(deg_all, 1)
                dve.wait_ge(deg_all, 1)
            tab2 = node_tab[:, :, :, :].rearrange("p g j t -> p (g j) t")
            all_dinv, all_half = tab2[:, :, 0], tab2[:, :, 1]
            link(nc.vector.tensor_scalar(all_half, sums2[:, :, 1], 1.0, None, ALU.max))
            link(nc.vector.reciprocal(all_half, all_half))
            link(nc.vector.tensor_scalar(all_half, all_half, 0.5, None, ALU.mult))
            link(nc.vector.tensor_scalar(nt_d[:, :], sums2[:, :, 0], 1.0, None, ALU.add))
            link(nc.vector.tensor_scalar(nt_a[:, :].bitcast(i32), nt_d[:, :].bitcast(i32), 1, None, ALU.arith_shift_right))
            link(nc.vector.tensor_scalar(nt_y[:, :].bitcast(i32), nt_a[:, :].bitcast(i32), -1.0, float(0x5f3759df), ALU.mult, ALU.add))
            for step in range(NEWTON):
                link(nc.vector.tensor_tensor(out=nt_a[:, :], in0=nt_y[:, :], in1=nt_y[:, :], op=ALU.mult))
                link(nc.vector.scalar_tensor_tensor(out=nt_a[:, :], in0=nt_a[:, :], scalar=-0.5, in1=nt_d[:, :], op0=ALU.mult, op1=ALU.mult))
                link(nc.vector.scalar_tensor_tensor(out=all_dinv if step == NEWTON - 1 else nt_y[:, :], in0=nt_a[:, :], scalar=1.5,
                                                    in1=nt_y[:, :], op0=ALU.add, op1=ALU.mult))
            for t in range(2):
                part = [node16[:, :, :, t, h].rearrange("p g j -> p (g j)") for h in range(PARTS)]
                link(nc.vector.tensor_copy(part[0], tab2[:, :, t]))
                link(nc.vector.tensor_tensor(out=nt_y[:, :], in0=tab2[:, :, t], in1=part[0], op=ALU.subtract))
                link(nc.vector.tensor_copy(part[1], nt_y[:, :]))
                link(nc.vector.tensor_tensor(out=part[2], in0=nt_y[:, :], in1=part[1], op=ALU.subtract))
            link(nc.vector.tensor_tensor(out=dinv2_tab[:, :, :].rearrange("p g j -> p (g j)"), in0=all_dinv, in1=all_dinv, op=ALU.mult))
            dve.sem_inc(dinv_ready, 1)

            def fe_copy(g, u, n):
                dve.wait_ge(fm_done.sem, fm_done.at(3, g))
                w = K * 2 * PARTS
                nc.vector.tensor_copy(xb_all[:, cut(g, w)], bank[2 + u % 4][:, 0:w]).then_inc(fe_done.sem, 1)

            run_steps(dve, [(4, fe_copy), (1, sT_of(3, fm_done))])
            dve.wait_ge(fe_done.sem, fe_done.at(3, NG - 1))
            fe_all = fe_parts.rearrange("p g k t h -> p (g k) t h")
            ew_all, simw_all, sim_all = (t[:, :, :].rearrange("p g k -> p (g k)") for t in (ew_tab, simw_tab, sim_tab))
            fe_sum = nt_a[:, 0:NG * K]
            for t, weight, to in ((0, ew_all, ew_all), (1, sim_all, simw_all)):
                link(nc.vector.tensor_tensor(out=fe_sum, in0=fe_all[:, :, t, 1], in1=fe_all[:, :, t, 2], op=ALU.add))
                link(nc.vector.tensor_tensor(out=fe_sum, in0=fe_all[:, :, t, 0], in1=fe_sum, op=ALU.add))
                link(nc.vector.tensor_tensor(out=to, in0=weight, in1=fe_sum, op=ALU.mult))

            walk_if_flagged(4)
            def x2_sum(g, u, n):
                dve.wait_ge(H_done.sem, H_done.at(4, g))
                if not early(g, 4):
                    dve.wait_ge(o_done.sem, o_done.at(4, g - 4))
                nc.vector.tensor_tensor(out=flat(hx, u % 4), in0=bank[2 + u % 4][:, 0:J * D], in1=flat(xa, u), op=ALU.add).then_inc(sum_done.sem, 1)

            outer = norm_out(4, sum_done, lambda u: hx[:, u % 4, :, :])
            run_steps(dve, [(6, outer.inverse), (5, outer.variance), (4, x2_sum), (0, S_of(4, ew_tab)), (6, outer.offset), (4, outer.sums)])
            walk_if_flagged(5)
            run_steps(dve, [(0, S_of(5, simw_tab))])
            dve.wait_ge(agg_done.sem, agg_done.at(5, NG - 1))
            walk_if_flagged(6)
            outer = norm_out(6, agg_done, lambda u: bj(u % 4))
            run_steps(dve, [(4, outer.inverse), (3, outer.sums), (0, S_of(6, simw_tab)), (4, outer.offset), (3, outer.variance)])

        @block.tensor
        def _(pe):
            pe.wait_ge(consts, 4)
            pe.wait_ge(cnt_done, 1)
            nc.tensor.matmul(bank[0][0:1, 0:NG + 1], ones_col[0:EP, :], cnt[:, :], start=True, stop=True).then_inc(e0_sum, 1)
            pe.wait_ge(flag_ready, 1)
            nc.tensor.matmul(bank[2][0:EP, 0:1], ones_row[:, 0:EP], flag_f[:, 0:1], start=True, stop=True).then_inc(flag_sum, 1)
            pe.wait_ge(weights_in, 16 * NW)
            nc.tensor.transpose(bank[1][:, 0:D], w_raw[:, :], ident[:, :]).then_inc(wsT_done, 1)
            pe.wait_ge(wsT_copied, 1)
            pe.wait_ge(e0_ready, 1)

            def msg_T_of(n, c, par, b):
                pe.wait_ge(gat_in[c % 4], b * (16 * EB // 4) + 16 * (c // 4 + 1))
                if c == 0:
                    pe.wait_ge(roh_ready, b + 1)
                if not early(n, 2):
                    pe.wait_ge(msg_Tc, n - 1)
                b_ = bank[7 * (c % 2)]
                nc.tensor.transpose(b_[:, 0:EP], gat[:, c % 4, :], ident[0:EP, 0:EP])
                nc.tensor.transpose(b_[0:R, P:P + EP], roh[:, par, c, :], ident[0:EP, 0:EP]).then_inc(msg_T, 1)

            def msg_Z_of(n, c2):
                pe.wait_ge(msg_Tc, n + 1)
                if not early(n, 2):
                    pe.wait_ge(msg_sel, n - 1)
                    pe.wait_ge(msg_act, n - 1)
                for q, (lo, hi) in enumerate(REL_CUT):
                    nc.tensor.matmul(bank[1 + q + 3 * c2][0:EP, 0:(hi - lo) * D], gatT[:, c2, :], w_rel[:, lo * D:hi * D], start=True, stop=True)
                nc.tensor.matmul(bank[3 + 3 * c2][0:EP, (R - REL_CUT[2][0]) * D:(R + 1 - REL_CUT[2][0]) * D], rohT[:, c2, :], b_rel[:, :],
                                 start=True, stop=True).then_inc(msg_Z, 1)

            def msg_steps(b, par, nb_):
                for c in range(EB):
                    msg_T_of(b * EB + c, c, par, b)
                    if not (early(b, 1) and c == 0):
                        msg_Z_of(b * EB + (c - 1), (c - 1) % 2)

            run_batches(pe, msg_steps)
            msg_Z_of(EC - 1, (EC - 1) % 2)

            flag = flagged(pe)
            pe.wait_ge(bias_in, 16 * J)

            def walk(p):
                with pe.Fori(0, EC) as c:
                    pe.wait_ge(one_diag, chunk(p, c) + 1)
                    nc.tensor.matmul(bank[1][0:EP, 0:EP], ones_sq, diag_n, start=True, stop=True).then_inc(one_bc, 1)
                    if p == 2:
                        pe.wait_ge(one_src, among((1, 2), p, c) * 16 + 16)
                        pe.wait_ge(one_dst, c * 16 + 16)
                        nc.tensor.transpose(bank[0][:, 0:EP], rows_s, ident[0:EP, 0:EP])
                        nc.tensor.transpose(bank[0][:, P:P + EP], rows_d, ident[0:EP, 0:EP]).then_inc(one_T, 1)
                        pe.wait_ge(one_Tc, c + 1)
                        nc.tensor.matmul(bank[4][0:H, 0:EP], mw1[:, 0, :], gT[:, 0, 0, 0:EP], start=True, stop=False)
                        nc.tensor.matmul(bank[4][0:H, 0:EP], mw1[:, 1, :], gT[:, 1, 0, 0:EP], start=False, stop=True).then_inc(one_hid, 1)
                        pe.wait_ge(one_hh, c + 1)
                        nc.tensor.matmul(bank[5][0:EP, 0:1], hh[:, 0, 0, 0:EP], mw2[:, :], start=True, stop=True).then_inc(one_log, 1)
                    pe.wait_ge(one_val, chunk(p, c) + 1)
                    nc.tensor.matmul(bank[2][0:EP, 0:D], same, val, start=True, stop=True).then_inc(one_sum, 1)

            def run_pass(p, stages):
                with pe.If(flag > 0):
                    walk(p)
                    run_steps(pe, stages(True))
                with pe.Else():
                    run_steps(pe, stages(False))

            def sums(p, with_extra):
                def stage(g, u, n):
                    pe.wait_ge(S_done.sem, S_done.at(p, g))
                    pe.wait_ge(xa_in[u], xa_count(p, u, n))
                    if p == 6:
                        pe.wait_ge(side_in[u], side_count(p, u, n))
                    pe.wait_ge(G_in[u], G_count(p, u, n))
                    if not early(g, 4):
                        pe.wait_ge(o_done.sem, o_done.at(p, g - 4))
                    if with_extra:
                        pe.wait_ge(xe_in[u % 4], xe_count(p, u, n))
                    for j in range(J):
                        nc.tensor.matmul(bj(u % 4)[:, j, :], half_ident[:, :], xa[:, u, j, :], start=True, stop=False)
                        if with_extra:
                            nc.tensor.matmul(bj(u % 4)[:, j, :], ident[:, :], xe[:, u % 4, j, :], start=False, stop=False)
                        if p == 6:
                            nc.tensor.matmul(bj(u % 4)[:, j, :], ident[:, :], xb[:, u, j, :], start=False, stop=False)
                        for k in range(K):
                            ins = nc.tensor.matmul(bj(u % 4)[:, j, :], S[:, u, k, j, :], G[:, u, k, :], start=False, stop=(k == K - 1))
                    ins.then_inc(agg_done.sem, 1)
                return stage

            def sums_flipped(p, with_extra):
                def stage(g, u, n):
                    pe.wait_ge(S_done.sem, S_done.at(p, g))
                    pe.wait_ge(xa_in[u], xa_count(p, u, n))
                    if p == 4:
                        pe.wait_ge(diag_done.sem, diag_done.at(4, g))
                    pe.wait_ge(G_in[u], G_count(p, u, n))
                    if not early(g, 2):
                        pe.wait_ge(Tc_done.sem, Tc_done.at(p, g - 2))
                    for k in range(K):
                        nc.tensor.matmul(bank[u % 2][:, 0:GN], G[:, u, k, :], flat_S(u, k), start=(k == 0), stop=False)
                    if with_extra:
                        pe.wait_ge(xe_in[u % 4], xe_count(p, u, n))
                        for j in range(J):
                            nc.tensor.matmul(bj(u % 2)[:, j, :], xe[:, u % 4, j, :], ident[:, :], start=False, stop=False)
                    for j in range(J):
                        ins = nc.tensor.matmul(bj(u % 2)[:, j, :], xa[:, u, j, :], r[:, u % 4, j, :] if p == 4 else ident[:, :],
                                               start=False, stop=(j == J - 1))
                    ins.then_inc(T_done.sem, 1)
                return stage

            def flip(g, u, n):
                pe.wait_ge(xa_in[u], xa_count(0, u, n))
                if not early(g, 2):
                    pe.wait_ge(Tc_done.sem, Tc_done.at(0, g - 2))
                for j in range(J):
                    ins = nc.tensor.transpose(bj(u % 2)[:, j, :], xa[:, u, j, :], ident[:, :])
                ins.then_inc(T_done.sem, 1)

            def self_and_messages(with_extra):
                def stage(g, u, n):
                    pe.wait_ge(Tc_done.sem, Tc_done.at(0, g))
                    pe.wait_ge(S_done.sem, S_done.at(0, g))
                    pe.wait_ge(side_in[u], side_count(0, u, n))
                    if not early(g, 4):
                        pe.wait_ge(n0_done.sem, n0_done.at(0, g - 4))
                    b_ = bank[2 + u % 4][:, 0:J * D]
                    nc.tensor.matmul(b_, ones16[:, :], bias_row(0), start=True, stop=False)
                    if with_extra:
                        pe.wait_ge(xe_in[u % 4], xe_count(0, u, n))
                    for j in range(J):
                        if with_extra:
                            nc.tensor.matmul(bj(2 + u % 4)[:, j, :], ident[:, :], xe[:, u % 4, j, :], start=False, stop=False)
                        nc.tensor.matmul(bj(2 + u % 4)[:, j, :], yT[:, u % 4, j, :], w_selfT[:, :], start=False, stop=False)
                        for k in range(K):
                            ins = nc.tensor.matmul(bj(2 + u % 4)[:, j, :], S[:, u, k, j, :], G[:, u, k, :], start=False, stop=(j == J - 1 and k == K - 1))
                    ins.then_inc(H_done.sem, 1)
                return stage

            run_pass(0, lambda extra_: [(1, flip), (3, self_and_messages(extra_))])

            def weighted(g, u, n):
                pe.wait_ge(Tc_done.sem, Tc_done.at(1, g))
                if not early(g, 2):
                    pe.wait_ge(sum_done.sem, sum_done.at(1, g - 2))
                nc.tensor.matmul(bank[2 + u % 2][:, 0:J * D], ones16[:, :], bias_row(1), start=True, stop=False)
                for j in range(J):
                    ins = nc.tensor.matmul(bj(2 + u % 2)[:, j, :], yT[:, u % 4, j, :], w1_sb[:, :], start=False, stop=(j == J - 1))
                ins.then_inc(H_done.sem, 1)

            run_pass(1, lambda extra_: [(1, sums_flipped(1, extra_)), (2, weighted)])

            def broadcast_dst(p):
                def stage(g, u, n):
                    pe.wait_ge(side_in[u], side_count(p, u, n))
                    if not early(g, 2):
                        pe.wait_ge(sT_done.sem, sT_done.at(p, g - 2))
                    nc.tensor.matmul(bank[6 + u % 2][:, 0:GE], ones16[0:2, :], drow[:, u, :], start=True, stop=True).then_inc(bc_done.sem, 1)
                return stage

            def flip_sources(g, u, n):
                pe.wait_ge(G_in[u], G_count(2, u, n))
                if not early(g, 1):
                    pe.wait_ge(Tc_done.sem, Tc_done.at(2, g - 1))
                for k in range(K):
                    ins = nc.tensor.transpose(bank[0][:, k * P:(k + 1) * P], G[:, u, k, :], ident[:, :])
                ins.then_inc(T_done.sem, 1)

            def dst_rows(g, u, n):
                pe.wait_ge(sT_done.sem, sT_done.at(2, g))
                pe.wait_ge(xa_in[u], xa_count(2, u, n))
                if not early(g, 1):
                    pe.wait_ge(xdc_done.sem, xdc_done.at(2, g - 1))
                for j in range(J):
                    ins = nc.tensor.matmul(bank[3][:, 0:GE], xa[:, u, j, :], sT[:, u % 2, j, :], start=(j == 0), stop=(j == J - 1))
                ins.then_inc(xd_done.sem, 1)

            def hidden(g, u, n):
                pe.wait_ge(Tc_done.sem, Tc_done.at(2, g))
                pe.wait_ge(xdc_done.sem, xdc_done.at(2, g))
                if not early(g, 1):
                    pe.wait_ge(hh_done.sem, hh_done.at(2, g - 1))
                nc.tensor.matmul(bank[4][0:H, 0:GE], mw1[:, 0, :], flat(gT, u % 4), start=True, stop=False)
                nc.tensor.matmul(bank[4][0:H, 0:GE].rearrange("h (k p) -> h k p", k=K), mw1[:, 1, :],
                                 xdT[:, u % 2, :].rearrange("d (p k) -> d k p", k=K), start=False, stop=True).then_inc(hp_done.sem, 1)

            def logits(g, u, n):
                pe.wait_ge(hh_done.sem, hh_done.at(2, g))
                if not early(g, 1):
                    pe.wait_ge(th_done.sem, th_done.at(2, g - 1))
                for k in range(K):
                    ins = nc.tensor.matmul(bank[5][:, k:k + 1], hh[:, u % 4, k, :], mw2[:, :], start=True, stop=True)
                ins.then_inc(ep_done.sem, 1)

            def degree_sums(g, u, n):
                pe.wait_ge(ew_done.sem, ew_done.at(2, g))
                if not early(g, 2):
                    pe.wait_ge(deg_done.sem, deg_done.at(2, g - 2))
                for j in range(J):
                    for k in range(K):
                        w = PARTS + 1
                        ins = nc.tensor.matmul(bank[1 + u % 2][:, w * j:w * (j + 1)], S16(u, k)[:, j, :], ew16[:, u % 4, k, :], start=(k == 0), stop=(k == K - 1))
                ins.then_inc(dg_done.sem, 1)

            with pe.If(flag > 0):
                walk(2)
            run_steps(pe, [(8, degree_sums), (5, logits), (4, hidden), (3, dst_rows), (2, flip_sources), (1, broadcast_dst(2))])

            pe.wait_ge(dinv_ready, 1)

            def look_up(g, u, n):
                pe.wait_ge(sT_done.sem, sT_done.at(3, g))
                if not early(g, 4):
                    pe.wait_ge(fe_done.sem, fe_done.at(3, g - 4))
                for k in range(K):
                    for j in range(J):
                        w = 2 * PARTS
                        tab = (node16[:, g, j, :, :].rearrange("p t h -> p (t h)") if isinstance(g, int)
                               else node16[:, bass.ds(g, 1), j, :, :].rearrange("p a t h -> p (a t h)"))
                        ins = nc.tensor.matmul(bank[2 + u % 4][:, w * k:w * (k + 1)],
                                               sT16(u, j).rearrange("p (e k) -> p k e", k=K)[:, k, :], tab, start=(j == 0), stop=(j == J - 1))
                ins.then_inc(fm_done.sem, 1)

            run_steps(pe, [(2, look_up), (0, broadcast_dst(3))])

            def convolved(g, u, n):
                pe.wait_ge(Tc_done.sem, Tc_done.at(4, g))
                if not early(g, 4):
                    pe.wait_ge(sum_done.sem, sum_done.at(4, g - 4))
                b_ = 2 + u % 4
                nc.tensor.matmul(bank[b_][:, 0:J * D], ones16[:, :], bias_row(2), start=True, stop=False)
                for j in range(J):
                    ins = nc.tensor.matmul(bj(b_)[:, j, :], yT[:, u % 4, j, :], cw[:, :], start=False, stop=(j == J - 1))
                ins.then_inc(H_done.sem, 1)

            run_pass(4, lambda extra_: [(2, sums_flipped(4, extra_)), (3, convolved)])
            run_pass(5, lambda extra_: [(2, sums(5, extra_))])
            run_pass(6, lambda extra_: [(2, sums(6, extra_))])


_INS = ["x", "src", "dst", "edge_attr_128", "edge_type_10", "L0_gnn_relation_weights", "L0_gnn_relation_bias",
        "L0_gnn_w_self", "L0_gnn_b_self", "L0_gnn_ln_gamma", "L0_gnn_ln_beta", "L1_gnn_W", "L1_gnn_b",
        "L2_gnn_mlp_w1", "L2_gnn_mlp_b1", "L2_gnn_mlp_w2", "L2_gnn_mlp_b2", "L2_gnn_conv_w", "L2_gnn_conv_b",
        "L3_gnn_question_emb"]


def kernel(**inputs):
    import numpy as _np
    import concourse.bacc as _bacc
    from concourse import mybir as _mybir
    from concourse.bass_utils import run_bass_kernel_spmd as _run

    nc = _bacc.Bacc("TRN2", target_bir_lowering=False, num_devices=1)
    arrays, args = {}, []
    for name in _INS:
        a = _np.ascontiguousarray(inputs[name])
        arrays[f"in_{name}_dram"] = a
        args.append(nc.dram_tensor(f"in_{name}_dram", a.shape, _mybir.dt.from_np(a.dtype), kind="ExternalInput").ap())
    shape = _np.asarray(inputs["x"]).shape
    args.append(nc.dram_tensor("out_0_dram", shape, _mybir.dt.float32, kind="ExternalOutput").ap())
    gnn_kernel(nc, *args)
    r = _run(nc, [arrays], core_ids=[0])
    return r.results[0]["out_0_dram"]
```
